# Optimizing a Trainium2 kernel written in Bass

```python
import numpy as np
import jax
import jax.numpy as jnp

def _softmax(x, axis=-1):
    return jax.nn.softmax(x, axis=axis)

def _gelu(x):
    return jax.nn.gelu(x, approximate=True)

def _silu(x):
    return jax.nn.silu(x)

def _sigmoid(x):
    return jax.nn.sigmoid(x)

def _layernorm(x, axis=-1, eps=1e-05):
    m = jnp.mean(x, axis=axis, keepdims=True)
    v = jnp.var(x, axis=axis, keepdims=True)
    return (x - m) / jnp.sqrt(v + eps)

def _scatter_add(tgt, idx, src, axis=0):
    return tgt.at[idx].add(src)

def _segment_sum(src, seg, n):
    return jax.ops.segment_sum(src, seg, n)
kernel_name = 'mk_adj_preln_d1_adj_r2_ddd8a1'

def setup_inputs(seed: int=0):
    np.random.seed(seed)
    _w = jnp.asarray

    def _rec_inputs():
        import jax
        import jax.numpy as jnp
        _gk = jax.random.key(seed)
        x = 7.22e-05 + 1 * jax.random.normal(jax.random.fold_in(_gk, 1), (64, 128, 128), jnp.float32)
        _a = jax.random.bernoulli(jax.random.fold_in(_gk, 2), 0.015625, (64, 128, 128))
        _a = jnp.logical_or(_a, jnp.swapaxes(_a, -1, -2))
        _a = jnp.logical_or(_a, jnp.eye(128, dtype=bool))
        _af = _a.astype(jnp.float32)
        adj = _af
        return (x, adj)
    x, adj = _rec_inputs()

    def _L0_gnn_setup():
        import jax, jax.numpy as jnp
        import numpy as np
        from jax import lax
        DIM = 128
        EPS = 1e-05

        def _bn(h, g, b, m, v):
            scale = g / jnp.sqrt(v + EPS)
            return h * scale[None, :, None] + (b - m * scale)[None, :, None]

        def _conv1d(h, w, pad):
            return lax.conv_general_dilated(h, w, window_strides=(1,), padding=[(pad, pad)], dimension_numbers=('NCH', 'OIH', 'NCH'))
        key = jax.random.key(seed)
        ks = jax.random.split(key, 16)
        bs, n, d = (16, 1024, DIM)
        s = 0.05
        return {'x': jax.random.normal(ks[0], (bs, n, d), jnp.float32), 'mask': jnp.ones((bs, n, n), jnp.float32), 'w_se': jax.random.normal(ks[1], (3, d), jnp.float32) * s, 'b_se': jnp.zeros((3,), jnp.float32), 'conv1_w': jax.random.normal(ks[2], (d, d, 1), jnp.float32) * s, 'bn1_g': jnp.ones((d,), jnp.float32), 'bn1_b': jnp.zeros((d,), jnp.float32), 'bn1_m': jnp.zeros((d,), jnp.float32), 'bn1_v': jnp.ones((d,), jnp.float32), 'conv2_w': jax.random.normal(ks[3], (d, d, 17), jnp.float32) * s, 'bn2_g': jnp.ones((d,), jnp.float32), 'bn2_b': jnp.zeros((d,), jnp.float32), 'bn2_m': jnp.zeros((d,), jnp.float32), 'bn2_v': jnp.ones((d,), jnp.float32), 'w_msg': jax.random.normal(ks[4], (d, d), jnp.float32) * s, 'b_msg': jnp.zeros((d,), jnp.float32), 'w_ih': jax.random.normal(ks[5], (3 * d, 2 * d), jnp.float32) * s, 'b_ih': jnp.zeros((3 * d,), jnp.float32), 'w_hh': jax.random.normal(ks[6], (3 * d, d), jnp.float32) * s, 'b_hh': jnp.zeros((3 * d,), jnp.float32)}
    _L0_gnn_all = _L0_gnn_setup()
    _L0_gnn_in = {k: v for k, v in _L0_gnn_all.items() if k in ('w_se', 'b_se', 'conv1_w', 'bn1_g', 'bn1_b', 'bn1_m', 'bn1_v', 'conv2_w', 'bn2_g', 'bn2_b', 'bn2_m', 'bn2_v', 'w_msg', 'b_msg', 'w_ih', 'b_ih', 'w_hh', 'b_hh')}
    del _L0_gnn_all
    return {'x': x, 'adj': adj, 'L0_gnn_w_se': _L0_gnn_in['w_se'], 'L0_gnn_b_se': _L0_gnn_in['b_se'], 'L0_gnn_conv1_w': _L0_gnn_in['conv1_w'], 'L0_gnn_bn1_g': _L0_gnn_in['bn1_g'], 'L0_gnn_bn1_b': _L0_gnn_in['bn1_b'], 'L0_gnn_bn1_m': _L0_gnn_in['bn1_m'], 'L0_gnn_bn1_v': _L0_gnn_in['bn1_v'], 'L0_gnn_conv2_w': _L0_gnn_in['conv2_w'], 'L0_gnn_bn2_g': _L0_gnn_in['bn2_g'], 'L0_gnn_bn2_b': _L0_gnn_in['bn2_b'], 'L0_gnn_bn2_m': _L0_gnn_in['bn2_m'], 'L0_gnn_bn2_v': _L0_gnn_in['bn2_v'], 'L0_gnn_w_msg': _L0_gnn_in['w_msg'], 'L0_gnn_b_msg': _L0_gnn_in['b_msg'], 'L0_gnn_w_ih': _L0_gnn_in['w_ih'], 'L0_gnn_b_ih': _L0_gnn_in['b_ih'], 'L0_gnn_w_hh': _L0_gnn_in['w_hh'], 'L0_gnn_b_hh': _L0_gnn_in['b_hh']}

def reference(x, adj, L0_gnn_w_se, L0_gnn_b_se, L0_gnn_conv1_w, L0_gnn_bn1_g, L0_gnn_bn1_b, L0_gnn_bn1_m, L0_gnn_bn1_v, L0_gnn_conv2_w, L0_gnn_bn2_g, L0_gnn_bn2_b, L0_gnn_bn2_m, L0_gnn_bn2_v, L0_gnn_w_msg, L0_gnn_b_msg, L0_gnn_w_ih, L0_gnn_b_ih, L0_gnn_w_hh, L0_gnn_b_hh):
    import jax
    import jax.numpy as jnp

    def _L0_gnn_ref(x, mask, w_se, b_se, conv1_w, bn1_g, bn1_b, bn1_m, bn1_v, conv2_w, bn2_g, bn2_b, bn2_m, bn2_v, w_msg, b_msg, w_ih, b_ih, w_hh, b_hh):
        import jax, jax.numpy as jnp
        import numpy as np
        from jax import lax
        DIM = 128
        EPS = 1e-05

        def _bn(h, g, b, m, v):
            scale = g / jnp.sqrt(v + EPS)
            return h * scale[None, :, None] + (b - m * scale)[None, :, None]

        def _conv1d(h, w, pad):
            return lax.conv_general_dilated(h, w, window_strides=(1,), padding=[(pad, pad)], dimension_numbers=('NCH', 'OIH', 'NCH'))
        d = x.shape[-1]
        xc = jnp.transpose(x, (0, 2, 1))
        h = _bn(_conv1d(xc, conv1_w, 0), bn1_g, bn1_b, bn1_m, bn1_v)
        h = jax.nn.relu(h)
        h = _bn(_conv1d(h, conv2_w, 8), bn2_g, bn2_b, bn2_m, bn2_v)
        x_conv = jnp.transpose(jax.nn.relu(h + xc), (0, 2, 1))
        s = x @ w_se.T + b_se
        sq = jnp.sum(s * s, axis=-1)
        dist = sq[:, :, None] + sq[:, None, :] - 2.0 * jnp.einsum('bnd,bmd->bnm', s, s)
        A = jnp.exp(-dist) * mask
        msg = jax.nn.relu(x @ w_msg.T + b_msg)
        x_nmp = jnp.einsum('bnm,bmd->bnd', A, msg)
        x_in = jnp.concatenate([x_conv, x_nmp], axis=-1)
        gi = x_in @ w_ih.T + b_ih
        gh = x @ w_hh.T + b_hh
        gi_r, gi_z, gi_n = (gi[..., :d], gi[..., d:2 * d], gi[..., 2 * d:])
        gh_r, gh_z, gh_n = (gh[..., :d], gh[..., d:2 * d], gh[..., 2 * d:])
        r = jax.nn.sigmoid(gi_r + gh_r)
        z = jax.nn.sigmoid(gi_z + gh_z)
        nn_ = jnp.tanh(gi_n + r * gh_n)
        return (1.0 - z) * nn_ + z * x
    h = jnp.maximum(_layernorm(x, axis=-1), 0.0)
    x = x + _L0_gnn_ref(h, adj, L0_gnn_w_se, L0_gnn_b_se, L0_gnn_conv1_w, L0_gnn_bn1_g, L0_gnn_bn1_b, L0_gnn_bn1_m, L0_gnn_bn1_v, L0_gnn_conv2_w, L0_gnn_bn2_g, L0_gnn_bn2_b, L0_gnn_bn2_m, L0_gnn_bn2_v, L0_gnn_w_msg, L0_gnn_b_msg, L0_gnn_w_ih, L0_gnn_b_ih, L0_gnn_w_hh, L0_gnn_b_hh)
    return x

_drawn_inputs = setup_inputs


def setup_inputs(seed=0):
    import zlib

    import numpy as np

    out = dict(_drawn_inputs(seed))
    spreads = {'L0_gnn_b_se': (0.0, 0.8),
     'L0_gnn_bn1_g': (1.0, 0.6),
     'L0_gnn_bn1_b': (0.0, 0.346),
     'L0_gnn_bn1_m': (0.0, 0.34),
     'L0_gnn_bn1_v': (1.0, 0.6),
     'L0_gnn_bn2_g': (1.0, 0.6),
     'L0_gnn_bn2_b': (0.0, 0.532),
     'L0_gnn_bn2_m': (0.0, 0.51),
     'L0_gnn_bn2_v': (1.0, 0.6),
     'L0_gnn_b_msg': (0.0, 0.1),
     'L0_gnn_b_ih': (0.0, 0.1),
     'L0_gnn_b_hh': (0.0, 0.34)}
    factors = {}
    for name, (base, spread) in spreads.items():
        noise = np.random.default_rng([zlib.crc32(name.encode()), seed]).standard_normal(out[name].shape)
        drawn = base * np.exp(spread * noise) if base else spread * noise
        out[name] = jnp.asarray(drawn.astype(out[name].dtype))
    for name, factor in factors.items():
        out[name] = (out[name] * factor).astype(out[name].dtype)
    return out
```

```python
from contextlib import ExitStack

import concourse.bass as bass
from concourse import mybir

F32 = mybir.dt.float32
F32R = mybir.dt.float32r
BF16 = mybir.dt.bfloat16
ALU = mybir.AluOpType
ACT = mybir.ActivationFunctionType
AX = mybir.AxisListType

EPS = 1e-5
GB = 4
QUAD = 32


def gnn_block(nc, x, adj, w_se, b_se, conv1_w, bn1_g, bn1_b, bn1_m, bn1_v, conv2_w, bn2_g, bn2_b, bn2_m, bn2_v,
              w_msg, b_msg, w_ih, b_ih, w_hh, b_hh, out):
    NB, N, D = x.shape
    NSE = w_se.shape[0]
    TAPS = conv2_w.shape[2]
    HALF = TAPS // 2
    NG = NB // GB
    GC = GB * N
    MS = D + NSE + 1
    UN = N // 2 + 1
    NPAD = 2 * UN
    UOFF = 2
    UPAD = UN + 5

    ctx = ExitStack()
    with ctx:
        def sb(name, shape, dt=F32):
            return ctx.enter_context(nc.sbuf_tensor(name, shape, dt))

        def sem(name):
            return ctx.enter_context(nc.semaphore(name))

        NVEC = 14 + NSE
        vecs = sb("vecs", [NVEC, D])
        vcol = sb("vcol", [D, NVEC])
        bn_rstd = sb("bn_rstd", [D, 2])
        bn_scale = sb("bn_scale", [D, 2])
        bn_ms = sb("bn_ms", [D, 2])
        bn_shift = sb("bn_shift", [D, 2])
        gru_b = sb("gru_b", [D, 4])
        gru_s = sb("gru_s", [D, 2])
        bias_row = sb("bias_row", [N, MS])
        c1_nat = sb("c1_nat", [D, D])
        c2_nat = sb("c2_nat", [D, D * TAPS])
        c2_sums = sb("c2_sums", [D, HALF, D])
        msg_nat = sb("msg_nat", [D, D])
        ih_nat = sb("ih_nat", [D, 3, 2 * D])
        hh_nat = sb("hh_nat", [D, 3, D])
        hhn_half = sb("hhn_half", [D, D])
        CONV1, CONV2, SUMS, HH = 0, 1, 1 + TAPS, 1 + TAPS + HALF
        IH, NMAT = HH + 3, HH + 9
        w_hi = sb("w_hi", [D, NMAT, D], F32R)
        w_lo = sb("w_lo", [D, NMAT, D], F32R)
        w_ms = sb("w_ms", [D, MS])
        ident = sb("ident", [128, 128])
        ident_b = sb("ident_b", [128, 128], BF16)
        halves = sb("halves", [128, 8])
        quad_mask = sb("quad_mask", [128, GB, N], BF16)

        x_all = sb("x_all", [N, NB, D])
        adj_in = [sb(f"adj_in{p}", [N, GB, N]) for p in range(2)]
        adj_T = sb("adj_T", [N, GC])
        stats = sb("stats", [N, GB, 6])
        halves_sum = sb("halves_sum", [N, GB])
        halves_diff = sb("halves_diff", [N, GB])
        diff_sq = sb("diff_sq", [N, GB])
        sq_sum = sb("sq_sum", [N, GB])
        sq_mean = sb("sq_mean", [N, GB])
        mean = sb("mean", [N, GB])
        var_eps = sb("var_eps", [N, GB])
        rstd = sb("rstd", [N, GB])
        x_norm = sb("x_norm", [N, GB, D])
        h_f = [sb(f"h_f{p}", [D, GC]) for p in range(2)]
        h_hi = [sb(f"h_hi{p}", [D, GC], F32R) for p in range(2)]
        h_lo = [sb(f"h_lo{p}", [D, GC], F32R) for p in range(2)]
        h_s = sb("h_s", [D, GC])
        h_keep = sb("h_keep", [D, GC])
        a1_f = sb("a1_f", [D, GB, NPAD])
        a1_sum = sb("a1_sum", [D, GB, UN])
        a1_hi = [sb(f"a1_hi{p}", [D, 3, GB, UPAD], F32R) for p in range(2)]
        a1_lo = [sb(f"a1_lo{p}", [D, 3, GB, UPAD], F32R) for p in range(2)]
        ms_b = sb("ms_b", [N, GB, MS])
        msg = sb("msg", [N, GB, D])
        s_sq = sb("s_sq", [N, GB, NSE])
        emb = sb("emb", [N, GB, NSE + 1])
        emb_rest = sb("emb_rest", [N, GB, NSE + 1])
        emb_part = sb("emb_part", [N, GB, 3, NSE + 1], BF16)
        dist_l = sb("dist_l", [N, GB, QUAD], BF16)
        dist_r = sb("dist_r", [N, GB, QUAD], BF16)
        dist_lT = sb("dist_lT", [128, GB, N], BF16)
        dist_rT = sb("dist_rT", [128, N], BF16)
        edge = sb("edge", [N, GC])
        edge_m = sb("edge_m", [N, GC])
        nmp_hi = [sb(f"nmp_hi{p}", [D, GC], F32R) for p in range(2)]
        nmp_lo = [sb(f"nmp_lo{p}", [D, GC], F32R) for p in range(2)]
        q0 = sb("q0", [D, GB, UN])
        q1 = sb("q1", [D, GB, N // 2])
        h_q0 = sb("h_q0", [D, GB, N // 2])
        q01 = sb("q01", [D, GB, N // 2])
        h_q01 = sb("h_q01", [D, GB, N // 2])
        conv_f = sb("conv_f", [D, GC])
        conv_hi = sb("conv_hi", [D, GC], F32R)
        conv_lo = sb("conv_lo", [D, GC], F32R)
        t_r = sb("t_r", [D, GC])
        t_z = sb("t_z", [D, GC])
        r2 = sb("r2", [D, GC])
        hn = sb("hn", [D, GC])
        n_pre = sb("n_pre", [D, GC])
        n_gate = sb("n_gate", [D, GC])
        diff = sb("diff", [D, GC])
        zdiff = sb("zdiff", [D, GC])
        gru = sb("gru", [D, GC])
        y = [sb(f"y{p}", [N, GB, D]) for p in range(2)]

        bank = [ctx.enter_context(nc.psum_tensor(f"bank{k}", [128, GC], F32)) for k in range(8)]
        B_CA, B_CB, B_R, B_Z, B_HN, B_N, B_F0, B_F1 = range(8)

        vecs_in, msgw_in, c1_in, c2_in, gruw_in, bias_in = (sem(n) for n in (
            "vecs_in", "msgw_in", "c1_in", "c2_in", "gruw_in", "bias_in"))
        x_in = [sem(f"x_in{p}") for p in range(2)]
        adj_in_sem = [sem(f"adj_in_sem{p}") for p in range(2)]
        out_done = [sem(f"out_done{p}") for p in range(2)]
        const_set = sem("const_set")
        dve_const = sem("dve_const")
        vecT_done, vcol_ready, bn_rstd_ready, bn_chain = (sem(n) for n in (
            "vecT_done", "vcol_ready", "bn_rstd_ready", "bn_chain"))
        c2_sums_ready, hhn_ready = sem("c2_sums_ready"), sem("hhn_ready")
        msgT_done, w_ms_ready = sem("msgT_done"), sem("w_ms_ready")
        wT_done, w_hi_ready, w_lo_ready = sem("wT_done"), sem("w_hi_ready"), sem("w_lo_ready")
        stats_ready = sem("stats_ready")
        parts_ready = sem("parts_ready")
        parts2_ready = sem("parts2_ready")
        mean_ready = sem("mean_ready")
        vareps_ready = sem("vareps_ready")
        rstd_ready = sem("rstd_ready")
        xnorm_ready = sem("xnorm_ready")
        hT_done = sem("hT_done")
        hf_ready, hhi_ready, hlo_ready = sem("hf_ready"), sem("hhi_ready"), sem("hlo_ready")
        conv1_done = sem("conv1_done")
        hs_ready, hkeep_ready = sem("hs_ready"), sem("hkeep_ready")
        a1f_ready, a1hi_ready, a1lo_ready = sem("a1f_ready"), sem("a1hi_ready"), sem("a1lo_ready")
        a1sum_ready, a1shi_ready, a1slo_ready = sem("a1sum_ready"), sem("a1shi_ready"), sem("a1slo_ready")
        msg_done = sem("msg_done")
        msb_ready = sem("msb_ready")
        msg_ready = sem("msg_ready")
        ssq_ready, emb_ready = sem("ssq_ready"), sem("emb_ready")
        part_ready, rest_ready = sem("part_ready"), sem("rest_ready")
        dist_in_ready = sem("dist_in_ready")
        distT_done = sem("distT_done")
        dlT_ready, drT_ready = sem("dlT_ready"), sem("drT_ready")
        adjT_ready = sem("adjT_ready")
        dist_done = sem("dist_done")
        edge_ready, edgem_ready = sem("edge_ready"), sem("edgem_ready")
        nmp_done, nmphi_ready, nmplo_ready = sem("nmp_done"), sem("nmphi_ready"), sem("nmplo_ready")
        q0_done, q1_done, q2_done = sem("q0_done"), sem("q1_done"), sem("q2_done")
        q0_ready, q1_ready = sem("q0_ready"), sem("q1_ready")
        hq0_ready, q01_ready, hq01_ready = sem("hq0_ready"), sem("q01_ready"), sem("hq01_ready")
        convf_ready, convhi_ready, convlo_ready = sem("convf_ready"), sem("convhi_ready"), sem("convlo_ready")
        gru_hn_done, gru_r_done, gru_z_done, gru_n_done = (sem(n) for n in (
            "gru_hn_done", "gru_r_done", "gru_z_done", "gru_n_done"))
        tr_ready, tz_ready, r2_ready, hn_ready, npre_ready = (sem(n) for n in (
            "tr_ready", "tz_ready", "r2_ready", "hn_ready", "npre_ready"))
        ngate_ready, diff_ready, zdiff_ready, gru_ready = (sem(n) for n in (
            "ngate_ready", "diff_ready", "zdiff_ready", "gru_ready"))
        outT_done, y_ready = sem("outT_done"), sem("y_ready")

        def wait(eng, s, value):
            if not (isinstance(value, int) and value <= 0):
                eng.wait_ge(s, value)

        def moved(g, p):
            return 8 * g + 16 - 8 * p

        def groups(eng, iteration):
            iteration(0, 0, True, False)
            iteration(1, 1, False, False)
            with eng.Fori(1, NG // 2 - 1) as pair:
                iteration(2 * pair, 0, False, False)
                iteration(2 * pair + 1, 1, False, False)
            iteration(NG - 2, 0, False, False)
            iteration(NG - 1, 1, False, True)

        def by_graph(ap):
            return ap.rearrange("p (b n) -> p b n", b=GB)

        def pairs_out(ap):
            return ap.rearrange("p (b u e) -> p b u e", b=GB, e=2)

        chunks = [[CONV1]] + [list(range(k, min(k + GB, NMAT))) for k in range(CONV2, NMAT, GB)]
        EARLY = sum(c[0] < HH for c in chunks)
        chunk_bank = [(B_CA, B_CB, B_N)[c % 3] if c < EARLY else B_N for c in range(len(chunks))]

        PAIRS = [(a, b) for a in range(3) for b in range(3 - a)]
        EMB = NSE + 1
        ONE_SLOT = len(PAIRS) * EMB
        DIST_OPS = 3 + 3 + 1
        DVE_CONSTS = 2 * 4 + 1 + 2 + 1 + 2 + 3 + GB
        QCOLS = (UN + 1, N // 2, N // 2)

        def conv_bank(p, k):
            return (B_CA, B_CB)[(p + k) % 2]

        block = ctx.enter_context(nc.Block())

        @block.sync
        def _(sp):
            def load_adj(g, p):
                for i in range(N // QUAD):
                    rows = slice(i * QUAD, (i + 1) * QUAD)
                    src = adj[bass.ds(g * GB, GB), :, rows].rearrange("b (j c) a -> c b j a", c=QUAD)
                    sp.dma_start(adj_in[p][rows, :, :].rearrange("c b (j a) -> c b j a", a=QUAD), src
                                 ).then_inc(adj_in_sem[p], 16)

            sp.dma_start(x_all[:, 0:GB, :], x[0:GB].rearrange("b n d -> n b d")).then_inc(x_in[0], 16)
            sp.dma_start(c1_nat[:, :], conv1_w.rearrange("o i k -> o (i k)")).then_inc(c1_in, 16)
            for row, src in enumerate((bn1_g, bn1_b, bn1_m, bn1_v, bn2_g, bn2_b, bn2_m, bn2_v)):
                sp.dma_start(vecs[row:row + 1, :], src.rearrange("(a d) -> a d", a=1)).then_inc(vecs_in, 16)
            sp.dma_start(vecs[8:11, :], b_ih.rearrange("(a d) -> a d", a=3)).then_inc(vecs_in, 16)
            sp.dma_start(vecs[11:14, :], b_hh.rearrange("(a d) -> a d", a=3)).then_inc(vecs_in, 16)
            sp.dma_start(vecs[14:NVEC, :], w_se).then_inc(vecs_in, 16)
            for p in range(2):
                load_adj(p, p)
            sp.dma_start(x_all[:, GB:2 * GB, :], x[GB:2 * GB].rearrange("b n d -> n b d")).then_inc(x_in[1], 16)

            def iteration(g, p, first, last):
                if not (isinstance(g, int) and g + 2 >= NG):
                    wait(sp, x_in[p], moved(g, p))
                    sp.dma_start(x_all[:, bass.ds((g + 2) * GB, GB), :],
                                 x[bass.ds((g + 2) * GB, GB)].rearrange("b n d -> n b d")).then_inc(x_in[p], 16)
                if not (isinstance(g, int) and g + 2 >= NG):
                    wait(sp, adjT_ready, g + 1)
                    load_adj(g + 2, p)
                if not first:
                    wait(sp, y_ready, g)
                    sp.dma_start(out[bass.ds((g - 1) * GB, GB)].rearrange("b n d -> n b d"), y[1 - p][:, :, :]
                                 ).then_inc(out_done[1 - p], 16)

            groups(sp, iteration)
            sp.wait_ge(y_ready, NG)
            sp.dma_start(out[(NG - 1) * GB:NG * GB].rearrange("b n d -> n b d"), y[(NG - 1) % 2][:, :, :]
                         ).then_inc(out_done[(NG - 1) % 2], 16)
            for p in range(2):
                sp.wait_ge(out_done[p], 16 * (NG // 2))

        @block.gpsimd
        def _(pool):
            pool.memset(ident[:, :], 0.0).then_inc(const_set, 1)
            pool.memset(halves[:, :], -0.5).then_inc(const_set, 1)
            pool.wait_ge(const_set, 2)
            pool.affine_select(out=ident[:, :], in_=ident[:, :], compare_op=ALU.not_equal, fill=1.0, base=0,
                               pattern=[[-1, 128]], channel_multiplier=1).then_inc(const_set, 1)

            pool.wait_ge(const_set, 3)
            pool.tensor_copy(ident_b[:, :], ident[:, :]).then_inc(const_set, 1)
            pool.dma_start(bias_row[:, 0:D], b_msg.partition_broadcast(N)).then_inc(bias_in, 16)
            pool.dma_start(bias_row[:, D:D + NSE], b_se.partition_broadcast(N)).then_inc(bias_in, 16)

            def norm_rstd(g):
                wait(pool, vareps_ready, g + 1)
                pool.tensor_tensor(rstd[:, :], var_eps[:, :], halves[:, 0:GB], ALU.pow).then_inc(rstd_ready, 1)

            def conv_parts(g):
                h_even, h_odd = (pairs_out(h_s[:, :])[:, :, :, e] for e in range(2))
                wait(pool, hs_ready, g + 1)
                wait(pool, convf_ready, 2 * g)
                wait(pool, q0_ready, g + 1)
                pool.tensor_tensor(h_q0[:, :, :], h_even, q0[:, :, 0:N // 2], ALU.add).then_inc(hq0_ready, 1)
                wait(pool, q1_ready, g + 1)
                pool.tensor_tensor(q01[:, :, :], q0[:, :, 1:UN], q1[:, :, :], ALU.add).then_inc(q01_ready, 1)
                wait(pool, q01_ready, g + 1)
                pool.tensor_tensor(h_q01[:, :, :], h_odd, q01[:, :, :], ALU.subtract).then_inc(hq01_ready, 1)

            norm_rstd(0)
            pool.dma_start(hh_nat[:, :, :], w_hh.rearrange("(a o) i -> o a i", a=3)).then_inc(gruw_in, 16)
            pool.dma_start(ih_nat[:, :, :], w_ih.rearrange("(a o) i -> o a i", a=3)).then_inc(gruw_in, 16)

            def tap_sums(half):
                js = slice(half * HALF // 2, (half + 1) * HALF // 2)
                pool.tensor_tensor(c2_sums[:, js, :], taps_nat[:, 0:TAPS - 1:2, :][:, js, :],
                                   taps_nat[:, 1:TAPS:2, :][:, js, :], ALU.add).then_inc(c2_sums_ready, 1)

            taps_nat = c2_nat[:, :].rearrange("o (i k) -> o k i", k=TAPS)
            pool.wait_ge(c2_in, 16)
            tap_sums(0)
            pool.wait_ge(vcol_ready, 1)
            pool.tensor_scalar(bn_rstd[:, :], vcol[:, 3:8:4], EPS, None, ALU.add).then_inc(bn_rstd_ready, 1)
            pool.wait_ge(bn_rstd_ready, 1)
            pool.tensor_tensor(bn_rstd[:, :], bn_rstd[:, :], halves[:, 0:2], ALU.pow).then_inc(bn_rstd_ready, 1)
            tap_sums(1)
            norm_rstd(1)

            def iteration(g, p, first, last):
                conv_parts(g)
                if not (isinstance(g, int) and g + 2 >= NG):
                    norm_rstd(g + 2)

            groups(pool, iteration)

        @block.scalar
        def _(act):
            act.dma_start(msg_nat[:, :], w_msg).then_inc(msgw_in, 16)
            act.dma_start(c2_nat[:, :], conv2_w.rearrange("o i k -> o (i k)")).then_inc(c2_in, 16)

            def weights_high(c):
                mats = chunks[c]
                act.wait_ge(wT_done, c + 1)
                act.activation(w_hi[:, mats[0]:mats[-1] + 1, :], bank[chunk_bank[c]][:, 0:len(mats) * D],
                               ACT.Copy).then_inc(w_hi_ready, 1)

            def h_copies(g, p):
                wait(act, hT_done, g + 1)
                wait(act, msg_done, 2 * (g - 1))
                wait(act, hlo_ready, g - 1)
                act.activation(h_f[p][:, :], bank[B_F0][:, :], ACT.Relu).then_inc(hf_ready, 1)
                wait(act, hf_ready, g + 1)
                act.activation(h_hi[p][:, :], h_f[p][:, :], ACT.Copy).then_inc(hhi_ready, 1)

            def conv1_out(g):
                wait(act, conv1_done, g + 1)
                wait(act, a1lo_ready, g)
                wait(act, a1sum_ready, g)
                act.activation(a1_f[:, :, 1:N + 1], by_graph(bank[B_F1][:, :]), ACT.Relu, bias=bn_shift[:, 0:1],
                               scale=bn_scale[:, 0:1]).then_inc(a1f_ready, 1)

            def a1_high(g, p):
                wait(act, a1f_ready, g + 1)
                wait(act, q2_done, g - 1)
                act.activation(a1_hi[p][:, 0:2, :, UOFF:UOFF + UN],
                               a1_f[:, :, :].rearrange("p b (u e) -> p e b u", e=2), ACT.Copy).then_inc(a1hi_ready, 1)

            def a1_sum_high(g, p):
                wait(act, a1sum_ready, g + 1)
                act.activation(a1_hi[p][:, 2, :, UOFF:UOFF + UN], a1_sum[:, :, :], ACT.Copy).then_inc(a1shi_ready, 1)

            def message_relu(g):
                wait(act, msb_ready, 2 * (g + 1))
                wait(act, nmp_done, g)
                act.activation(msg[:, :, :], ms_b[:, :, 0:D], ACT.Relu).then_inc(msg_ready, 1)

            def dist_right(g):
                wait(act, distT_done, g + 1)
                wait(act, dist_done, g)
                act.activation(dist_rT[:, :], bank[B_F1][:, 0:N // 2].bitcast(BF16), ACT.Copy).then_inc(drT_ready, 1)

            def edges(g):
                wait(act, dist_done, g + 1)
                wait(act, edgem_ready, g)
                act.activation(edge[:, :], bank[B_Z][:, :], ACT.Exp).then_inc(edge_ready, 1)

            def nmp_high(g, p):
                wait(act, nmp_done, g + 1)
                wait(act, gru_n_done, g - 1)
                act.activation(nmp_hi[p][:, :], bank[B_F0][:, :], ACT.Copy).then_inc(nmphi_ready, 1)

            def h_shifted(g, p):
                wait(act, hq01_ready, g)
                act.activation(h_s[:, :], h_f[p][:, :], ACT.Identity, bias=bn_shift[:, 1:2]).then_inc(hs_ready, 1)
                wait(act, diff_ready, g)
                act.activation(h_keep[:, :], h_f[p][:, :], ACT.Copy).then_inc(hkeep_ready, 1)

            def q0_scaled(g, p):
                wait(act, q0_done, g + 1)
                wait(act, hq01_ready, g)
                src = bank[conv_bank(p, 0)][:, 0:GB * QCOLS[0]].rearrange("p (b u) -> p b u", b=GB)
                act.activation(q0[:, :, :], src[:, :, 0:UN], ACT.Copy, scale=bn_scale[:, 1:2]).then_inc(q0_ready, 1)

            def q1_scaled(g, p):
                wait(act, q1_done, g + 1)
                wait(act, convf_ready, 2 * g)
                src = bank[conv_bank(p, 1)][:, 0:GB * QCOLS[1]].rearrange("p (b u) -> p b u", b=GB)
                act.activation(q1[:, :, :], src, ACT.Copy, scale=bn_scale[:, 1:2]).then_inc(q1_ready, 1)

            def conv_high(g):
                wait(act, convf_ready, 2 * (g + 1))
                wait(act, gru_n_done, g)
                act.activation(conv_hi[:, :], conv_f[:, :], ACT.Relu).then_inc(convhi_ready, 1)

            def gates_rz(g):
                wait(act, gru_r_done, g + 1)
                wait(act, r2_ready, g)
                act.activation(t_r[:, :], bank[B_R][:, :], ACT.Tanh, bias=gru_b[:, 0:1], scale=0.5).then_inc(tr_ready, 1)
                wait(act, gru_z_done, g + 1)
                wait(act, zdiff_ready, g)
                act.activation(t_z[:, :], bank[B_Z][:, :], ACT.Tanh, bias=gru_b[:, 1:2], scale=0.5).then_inc(tz_ready, 1)

            def gate_n(g):
                wait(act, npre_ready, g + 1)
                wait(act, gru_ready, g)
                act.activation(n_gate[:, :], n_pre[:, :], ACT.Tanh, bias=gru_b[:, 3:4]).then_inc(ngate_ready, 1)

            weights_high(0)
            weights_high(1)
            h_copies(0, 0)
            weights_high(2)
            act.wait_ge(bn_chain, 7)
            act.wait_ge(dve_const, DVE_CONSTS)
            conv1_out(0)
            message_relu(0)
            weights_high(3)
            a1_high(0, 0)
            dist_right(0)
            weights_high(4)
            edges(0)
            a1_sum_high(0, 0)
            weights_high(5)
            weights_high(6)
            for c in range(7, EARLY):
                weights_high(c)
            nmp_high(0, 0)

            def iteration(g, p, first, last):
                q = 1 - p
                if not first:
                    gates_rz(g - 1)
                if not last:
                    h_copies(g + 1, q)
                if not first:
                    gate_n(g - 1)
                if not last:
                    conv1_out(g + 1)
                if first:
                    weights_high(EARLY)
                if not last:
                    a1_high(g + 1, q)
                    message_relu(g + 1)
                    dist_right(g + 1)
                q0_scaled(g, p)
                if not last:
                    edges(g + 1)
                if first:
                    weights_high(EARLY + 1)
                h_shifted(g, p)
                q1_scaled(g, p)
                if not last:
                    a1_sum_high(g + 1, q)
                if not last:
                    nmp_high(g + 1, q)
                conv_high(g)

            groups(act, iteration)
            gates_rz(NG - 1)
            gate_n(NG - 1)

        @block.vector
        def _(dve):
            for t in a1_hi + a1_lo:
                dve.memset(t[:, :, :, 0:UOFF].bitcast(F32), 0.0).then_inc(dve_const, 1)
                dve.memset(t[:, :, :, UOFF + UN:UPAD].bitcast(F32), 0.0).then_inc(dve_const, 1)
            dve.memset(a1_f[:, :, 0:NPAD:NPAD - 1], 0.0).then_inc(dve_const, 1)
            for t in (dist_l, dist_r):
                dve.memset(t[:, :, :], 0.0).then_inc(dve_const, 1)
            dve.memset(quad_mask[:, :, :], 0.0).then_inc(dve_const, 1)
            dve.memset(w_ms[:, D + NSE:MS], 0.0).then_inc(dve_const, 1)
            dve.memset(bias_row[:, D + NSE:MS], 0.0).then_inc(dve_const, 1)
            dve.wait_ge(dve_const, DVE_CONSTS - 4 - GB)
            dve.memset(dist_l[:, :, ONE_SLOT:ONE_SLOT + 3], 1.0).then_inc(dve_const, 1)
            for k, (a, b) in enumerate(PAIRS):
                if b == 0:
                    dve.memset(dist_r[:, :, k * EMB + NSE], -1.0).then_inc(dve_const, 1)
            for b in range(GB):
                dve.memset(quad_mask[b * QUAD:(b + 1) * QUAD, b, :], 1.0).then_inc(dve_const, 1)

            def x_stats(g, p):
                wait(dve, x_in[p], moved(g, p))
                for b in range(GB):
                    dve.bn_stats(stats[:, b, :], x_all[:, bass.ds(g * GB + b, 1), :]).then_inc(stats_ready, 1)
                wait(dve, stats_ready, GB * (g + 1))
                even, odd = stats[:, :, 1], stats[:, :, 4]
                dve.tensor_tensor(halves_sum[:, :], even, odd, ALU.add).then_inc(parts_ready, 1)
                dve.tensor_tensor(halves_diff[:, :], even, odd, ALU.subtract).then_inc(parts_ready, 1)
                dve.tensor_tensor(sq_sum[:, :], stats[:, :, 2], stats[:, :, 5], ALU.add).then_inc(parts_ready, 1)
                wait(dve, parts_ready, 3 * (g + 1))
                dve.tensor_tensor(diff_sq[:, :], halves_diff[:, :], halves_diff[:, :], ALU.mult
                                  ).then_inc(parts2_ready, 1)
                dve.tensor_scalar(sq_mean[:, :], sq_sum[:, :], 1.0 / D, EPS, ALU.mult, ALU.add
                                  ).then_inc(parts2_ready, 1)
                dve.tensor_scalar(mean[:, :], halves_sum[:, :], 0.5, None, ALU.mult).then_inc(mean_ready, 1)
                wait(dve, parts2_ready, 2 * (g + 1))
                dve.scalar_tensor_tensor(var_eps[:, :], diff_sq[:, :], 0.25, sq_mean[:, :], ALU.mult, ALU.add
                                         ).then_inc(vareps_ready, 1)

            def x_normed(g):
                wait(dve, mean_ready, g + 1)
                wait(dve, rstd_ready, g + 1)
                for b in range(GB):
                    dve.tensor_scalar(x_norm[:, b:b + 1, :], x_all[:, bass.ds(g * GB + b, 1), :],
                                      mean[:, b:b + 1], rstd[:, b:b + 1], ALU.subtract, ALU.mult
                                      ).then_inc(xnorm_ready, 1)

            def h_low(g, p):
                wait(dve, hhi_ready, g + 1)
                dve.tensor_tensor(h_lo[p][:, :], h_f[p][:, :], h_hi[p][:, :].bitcast(F32), ALU.subtract
                                  ).then_inc(hlo_ready, 1)

            def a1_low(g, p):
                wait(dve, a1hi_ready, g + 1)
                for e in range(2):
                    low = dve.tensor_tensor(a1_lo[p][:, e, :, UOFF:UOFF + UN], a1_f[:, :, e:NPAD:2],
                                            a1_hi[p][:, e, :, UOFF:UOFF + UN].bitcast(F32), ALU.subtract)
                low.then_inc(a1lo_ready, 1)
                wait(dve, a1slo_ready, g)
                dve.tensor_tensor(a1_sum[:, :, :], a1_f[:, :, 0:NPAD:2], a1_f[:, :, 1:NPAD:2], ALU.add
                                  ).then_inc(a1sum_ready, 1)

            def a1_sum_low(g, p):
                wait(dve, a1shi_ready, g + 1)
                dve.tensor_tensor(a1_lo[p][:, 2, :, UOFF:UOFF + UN], a1_sum[:, :, :],
                                  a1_hi[p][:, 2, :, UOFF:UOFF + UN].bitcast(F32), ALU.subtract
                                  ).then_inc(a1slo_ready, 1)

            def messages(g):
                half = GB // 2
                wait(dve, msg_ready, g)
                for k, src in enumerate((B_HN, B_F0)):
                    wait(dve, msg_done, 2 * g + k + 1)
                    dve.tensor_tensor(ms_b[:, k * half:(k + 1) * half, :],
                                      bank[src][:, 0:half * MS].rearrange("p (b m) -> p b m", b=half),
                                      bias_row[:, :].unsqueeze(1).broadcast_to([N, half, MS]), ALU.add
                                      ).then_inc(msb_ready, 1)

            def dist_sides(g):
                e = ms_b[:, :, D:D + NSE]
                wait(dve, msb_ready, 2 * (g + 1))
                dve.tensor_tensor(s_sq[:, :, :], e, e, ALU.mult).then_inc(ssq_ready, 1)
                dve.tensor_copy(emb[:, :, 0:NSE], e).then_inc(emb_ready, 1)
                wait(dve, ssq_ready, g + 1)
                dve.tensor_reduce(emb[:, :, NSE:EMB], s_sq[:, :, :], AX.X, ALU.add).then_inc(emb_ready, 1)
                wait(dve, emb_ready, 2 * (g + 1))
                dve.tensor_copy(emb_part[:, :, 0, :], emb[:, :, :]).then_inc(part_ready, 1)
                wait(dve, part_ready, 3 * g + 1)
                dve.tensor_tensor(emb_rest[:, :, :], emb[:, :, :], emb_part[:, :, 0, :], ALU.subtract
                                  ).then_inc(rest_ready, 1)
                dve.tensor_copy(dist_l[:, :, 0:3 * EMB].rearrange("n b (k e) -> n b k e", k=3),
                                emb_part[:, :, 0:1, :].broadcast_to([N, GB, 3, EMB])).then_inc(dist_in_ready, 1)
                wait(dve, rest_ready, g + 1)
                dve.tensor_copy(emb_part[:, :, 1, :], emb_rest[:, :, :]).then_inc(part_ready, 1)
                wait(dve, part_ready, 3 * g + 2)
                dve.tensor_tensor(emb_part[:, :, 2, :], emb_rest[:, :, :], emb_part[:, :, 1, :], ALU.subtract
                                  ).then_inc(part_ready, 1)
                dve.tensor_copy(dist_l[:, :, 3 * EMB:5 * EMB].rearrange("n b (k e) -> n b k e", k=2),
                                emb_part[:, :, 1:2, :].broadcast_to([N, GB, 2, EMB])).then_inc(dist_in_ready, 1)
                right = dist_r[:, :, 0:6 * EMB].rearrange("n b (k e) -> n b k e", k=6)
                dve.tensor_scalar(right[:, :, 3:5, 0:NSE], emb_part[:, :, 0:2, 0:NSE], 2.0, None, ALU.mult
                                  ).then_inc(dist_in_ready, 1)
                dve.tensor_scalar(right[:, :, 5, 0:NSE], emb_part[:, :, 0, 0:NSE], 2.0, None, ALU.mult
                                  ).then_inc(dist_in_ready, 1)
                wait(dve, part_ready, 3 * (g + 1))
                dve.tensor_copy(dist_l[:, :, 5 * EMB:6 * EMB], emb_part[:, :, 2, :]).then_inc(dist_in_ready, 1)
                dve.tensor_scalar(right[:, :, 0:3, 0:NSE], emb_part[:, :, :, 0:NSE], 2.0, None, ALU.mult
                                  ).then_inc(dist_in_ready, 1)
                dve.tensor_scalar(dist_r[:, :, ONE_SLOT:ONE_SLOT + 3], emb_part[:, :, :, NSE], -1.0, None, ALU.mult
                                  ).then_inc(dist_in_ready, 1)

            def dist_left(g):
                wait(dve, distT_done, g + 1)
                dve.tensor_tensor(dist_lT[:, :, :], bank[B_F0][:, 0:N // 2].bitcast(BF16).unsqueeze(1).broadcast_to([128, GB, N]),
                                  quad_mask[:, :, :], ALU.mult).then_inc(dlT_ready, 1)

            def adj_transposed(g, p):
                wait(dve, adj_in_sem[p], N // QUAD * moved(g, p))
                dve.transpose(adj_T[:, :], adj_in[p][:, :, :].rearrange("n b m -> n (b m)")).then_inc(adjT_ready, 1)

            def masked_edges(g):
                wait(dve, adjT_ready, g + 1)
                wait(dve, edge_ready, g + 1)
                dve.tensor_tensor(edge_m[:, :], adj_T[:, :], edge[:, :], ALU.mult).then_inc(edgem_ready, 1)

            def nmp_low(g, p):
                wait(dve, nmphi_ready, g + 1)
                dve.tensor_tensor(nmp_lo[p][:, :], bank[B_F0][:, :], nmp_hi[p][:, :].bitcast(F32), ALU.subtract
                                  ).then_inc(nmplo_ready, 1)

            def conv_even(g):
                wait(dve, hq0_ready, g + 1)
                wait(dve, q1_ready, g + 1)
                dve.tensor_tensor(pairs_out(conv_f[:, :])[:, :, :, 0], h_q0[:, :, :], q1[:, :, :], ALU.add
                                  ).then_inc(convf_ready, 1)

            def conv_odd(g, p):
                wait(dve, hq01_ready, g + 1)
                wait(dve, q2_done, g + 1)
                src = bank[conv_bank(p, 2)][:, 0:GB * QCOLS[2]].rearrange("p (b u) -> p b u", b=GB)
                dve.scalar_tensor_tensor(pairs_out(conv_f[:, :])[:, :, :, 1], src, bn_scale[:, 1:2], h_q01[:, :, :],
                                         ALU.mult, ALU.add).then_inc(convf_ready, 1)

            def conv_low(g):
                wait(dve, convhi_ready, g + 1)
                dve.scalar_tensor_tensor(conv_lo[:, :], conv_f[:, :], 0.0, conv_hi[:, :].bitcast(F32),
                                         ALU.max, ALU.subtract).then_inc(convlo_ready, 1)

            def gate_pre(g):
                wait(dve, tr_ready, g + 1)
                dve.tensor_scalar(r2[:, :], t_r[:, :], 1.0, None, ALU.add).then_inc(r2_ready, 1)
                wait(dve, gru_hn_done, g + 1)
                wait(dve, r2_ready, g + 1)
                dve.scalar_tensor_tensor(hn[:, :], bank[B_HN][:, :], gru_b[:, 2:3], r2[:, :], ALU.add, ALU.mult
                                         ).then_inc(hn_ready, 1)
                wait(dve, gru_n_done, g + 1)
                wait(dve, hn_ready, g + 1)
                dve.tensor_tensor(n_pre[:, :], bank[B_N][:, :], hn[:, :], ALU.add).then_inc(npre_ready, 1)

            def gate_out(g):
                wait(dve, ngate_ready, g + 1)
                wait(dve, hkeep_ready, g + 1)
                dve.tensor_tensor(diff[:, :], h_keep[:, :], n_gate[:, :], ALU.subtract).then_inc(diff_ready, 1)
                wait(dve, tz_ready, g + 1)
                wait(dve, diff_ready, g + 1)
                dve.scalar_tensor_tensor(zdiff[:, :], t_z[:, :], 1.0, diff[:, :], ALU.add, ALU.mult
                                         ).then_inc(zdiff_ready, 1)
                wait(dve, zdiff_ready, g + 1)
                dve.scalar_tensor_tensor(gru[:, :], zdiff[:, :], 0.5, n_gate[:, :], ALU.mult, ALU.add
                                         ).then_inc(gru_ready, 1)

            def result(g, p):
                wait(dve, outT_done, g + 1)
                wait(dve, out_done[p], moved(g, p) - 16)
                dve.tensor_tensor(y[p][:, :, :], by_graph(bank[B_N][:, :]), x_all[:, bass.ds(g * GB, GB), :],
                                  ALU.add).then_inc(y_ready, 1)

            def weights_low(c):
                part = slice(chunks[c][0], chunks[c][-1] + 1)
                dve.wait_ge(w_hi_ready, c + 1)
                dve.tensor_tensor(w_lo[:, part, :],
                                  bank[chunk_bank[c]][:, 0:len(chunks[c]) * D].rearrange("p (m d) -> p m d", d=D),
                                  w_hi[:, part, :].bitcast(F32), ALU.subtract).then_inc(w_lo_ready, 1)

            x_stats(0, 0)
            dve.wait_ge(msgT_done, 1)
            dve.tensor_copy(w_ms[:, 0:D], bank[B_F1][:, D:2 * D]).then_inc(w_ms_ready, 1)
            weights_low(0)
            x_normed(0)
            weights_low(1)
            dve.wait_ge(vecT_done, 1)
            dve.tensor_copy(vcol[:, :], bank[B_F1][:, 0:NVEC]).then_inc(vcol_ready, 1)
            dve.wait_ge(vcol_ready, 1)
            dve.tensor_copy(w_ms[:, D:D + NSE], vcol[:, 14:NVEC]).then_inc(w_ms_ready, 1)
            dve.tensor_tensor(gru_s[:, :], vcol[:, 8:10], vcol[:, 11:13], ALU.add).then_inc(bn_chain, 1)
            dve.tensor_scalar(gru_b[:, 2:3], vcol[:, 13:14], 0.5, None, ALU.mult).then_inc(bn_chain, 1)
            dve.tensor_copy(gru_b[:, 3:4], vcol[:, 10:11]).then_inc(bn_chain, 1)
            dve.wait_ge(bn_chain, 3)
            dve.tensor_scalar(gru_b[:, 0:2], gru_s[:, :], 0.5, None, ALU.mult).then_inc(bn_chain, 1)
            dve.wait_ge(bn_rstd_ready, 2)
            dve.tensor_tensor(bn_scale[:, :], vcol[:, 0:8:4], bn_rstd[:, :], ALU.mult).then_inc(bn_chain, 1)
            dve.wait_ge(bn_chain, 5)
            dve.tensor_tensor(bn_ms[:, :], vcol[:, 2:8:4], bn_scale[:, :], ALU.mult).then_inc(bn_chain, 1)
            dve.wait_ge(bn_chain, 6)
            dve.tensor_tensor(bn_shift[:, :], vcol[:, 1:8:4], bn_ms[:, :], ALU.subtract).then_inc(bn_chain, 1)
            dve.wait_ge(gruw_in, 32)
            dve.tensor_scalar(hhn_half[:, :], hh_nat[:, 2, :], 0.5, None, ALU.mult).then_inc(hhn_ready, 1)
            h_low(0, 0)
            weights_low(2)
            dve.wait_ge(bias_in, 32)
            dve.wait_ge(dve_const, DVE_CONSTS)
            messages(0)
            dist_sides(0)
            dist_left(0)
            a1_low(0, 0)
            weights_low(3)
            weights_low(4)
            adj_transposed(0, 0)
            masked_edges(0)
            a1_sum_low(0, 0)
            weights_low(5)
            weights_low(6)
            for c in range(7, EARLY):
                weights_low(c)
            x_stats(1, 1)
            nmp_low(0, 0)
            x_normed(1)

            def iteration(g, p, first, last):
                q = 1 - p
                before_last_two = not (isinstance(g, int) and g + 2 >= NG)
                if not first:
                    gate_pre(g - 1)
                if not last:
                    h_low(g + 1, q)
                    messages(g + 1)
                    dist_sides(g + 1)
                if first:
                    weights_low(EARLY)
                if not first:
                    gate_out(g - 1)
                if not last:
                    dist_left(g + 1)
                    a1_low(g + 1, q)
                    adj_transposed(g + 1, q)
                    masked_edges(g + 1)
                if first:
                    weights_low(EARLY + 1)
                if before_last_two:
                    x_stats(g + 2, p)
                conv_even(g)
                if not last:
                    a1_sum_low(g + 1, q)
                conv_odd(g, p)
                if not first:
                    result(g - 1, q)
                conv_low(g)
                if not last:
                    nmp_low(g + 1, q)
                if before_last_two:
                    x_normed(g + 2)

            groups(dve, iteration)
            gate_pre(NG - 1)
            gate_out(NG - 1)
            result(NG - 1, (NG - 1) % 2)

        @block.tensor
        def _(pe):
            def split_product(out, mat, hi, lo, start, stop, done=None):
                pe.matmul(out, w_hi[:, mat, :], hi, start=start, stop=False)
                pe.matmul(out, w_hi[:, mat, :], lo, start=False, stop=False)
                last = pe.matmul(out, w_lo[:, mat, :], hi, start=False, stop=stop)
                if done is not None:
                    last.then_inc(done, 1)

            def conv2_taps(g, p, k, first, last):
                parity = (0, 1, 0)[k]
                kind = (1, 0, 2)[k]
                have = ((0, UN - 1), (1, UN), (0, UN))[k]
                start = (0, 1, 1)[k]
                steps = len(range(parity, TAPS, 2))
                order = sorted(range(steps), key=lambda j: abs(j - HALF // 2))
                dst = bank[conv_bank(p, k)][:, 0:GB * QCOLS[k]].rearrange("p (b u) -> p b u", b=GB)
                if first == 0:
                    if k == 0:
                        wait(pe, a1hi_ready, g + 1)
                        wait(pe, a1lo_ready, g + 1)
                        wait(pe, q1_ready, g)
                    elif k == 1:
                        wait(pe, convf_ready, 2 * g)
                    else:
                        wait(pe, a1shi_ready, g + 1)
                        wait(pe, a1slo_ready, g + 1)
                        wait(pe, q0_ready, g + 1)
                for j in order[first:last]:
                    shift = j - HALF // 2
                    lo = max(0, have[0] - shift - start) // 2 * 2
                    hi = min(QCOLS[k], (have[1] - shift - start + 1) // 2 * 2)
                    if shift == 0:
                        lo, hi = 0, QCOLS[k]
                    cols = slice(lo + start + shift + UOFF, hi + start + shift + UOFF)
                    mat = SUMS + j if k == 2 and j < HALF else CONV2 + 2 * j + parity
                    split_product(dst[:, :, lo:hi], mat, a1_hi[p][:, kind, :, cols], a1_lo[p][:, kind, :, cols],
                                  j == order[0], j == order[-1], (q0_done, q1_done, q2_done)[k]
                                  if j == order[-1] else None)

            def h_transposes(g):
                wait(pe, xnorm_ready, GB * (g + 1))
                wait(pe, nmplo_ready, g)
                for b in range(GB):
                    t = pe.transpose(bank[B_F0][:, b * N:(b + 1) * N], x_norm[:, b, :], ident[:, :])
                t.then_inc(hT_done, 1)

            def conv1(g, p):
                wait(pe, hhi_ready, g + 1)
                wait(pe, hlo_ready, g + 1)
                wait(pe, drT_ready, g)
                split_product(bank[B_F1][:, :], CONV1, h_hi[p][:, :], h_lo[p][:, :], True, True, conv1_done)

            def messages(g, p):
                half = GB // 2
                wait(pe, hf_ready, g + 1)
                wait(pe, hn_ready, g - 1)
                for k, dst in enumerate((B_HN, B_F0)):
                    for b in range(half):
                        m = pe.matmul(bank[dst][:, b * MS:(b + 1) * MS],
                                      h_f[p][:, (k * half + b) * N:(k * half + b + 1) * N], w_ms[:, :],
                                      start=True, stop=True)
                    m.then_inc(msg_done, 1)

            def dist_transposes(g):
                wait(pe, dist_in_ready, DIST_OPS * (g + 1))
                wait(pe, a1f_ready, g + 1)
                pe.transpose(bank[B_F0][:, 0:N // 2].bitcast(BF16), dist_l[:, :, :].rearrange("n b k -> n (b k)"),
                             ident_b[:, :])
                pe.transpose(bank[B_F1][:, 0:N // 2].bitcast(BF16), dist_r[:, :, :].rearrange("n b k -> n (b k)"),
                             ident_b[:, :]
                             ).then_inc(distT_done, 1)

            def distances(g):
                wait(pe, dlT_ready, g + 1)
                wait(pe, drT_ready, g + 1)
                wait(pe, tz_ready, g - 1)
                for b in range(GB):
                    m = pe.matmul(bank[B_Z][:, b * N:(b + 1) * N], dist_lT[:, b, :], dist_rT[:, :],
                                  start=True, stop=True)
                m.then_inc(dist_done, 1)

            def aggregate(g):
                wait(pe, msg_ready, g + 1)
                wait(pe, edgem_ready, g + 1)
                wait(pe, dlT_ready, g + 1)
                for b in range(GB):
                    m = pe.matmul(bank[B_F0][:, b * N:(b + 1) * N], msg[:, b, :], edge_m[:, b * N:(b + 1) * N],
                                  start=True, stop=True)
                m.then_inc(nmp_done, 1)

            def gru_products(g, p, first, last):
                h, nmp, conv = (h_hi[p], h_lo[p]), (nmp_hi[p], nmp_lo[p]), (conv_hi, conv_lo)

                def part(dst, mat, act, start, stop, done=None):
                    split_product(bank[dst][:, :], mat, act[0][:, :], act[1][:, :], start, stop, done)

                if last:
                    wait(pe, hn_ready, g)
                    wait(pe, tr_ready, g)
                    wait(pe, tz_ready, g)
                else:
                    wait(pe, msb_ready, 2 * (g + 2))
                    wait(pe, tr_ready, g)
                    wait(pe, edge_ready, g + 2)
                wait(pe, nmplo_ready, g + 1)
                part(B_HN, HH + 2, h, True, True, gru_hn_done)
                part(B_R, HH, h, True, False)
                part(B_R, IH + 1, nmp, False, False)
                part(B_Z, HH + 1, h, True, False)
                part(B_Z, IH + 3, nmp, False, False)
                wait(pe, y_ready, g)
                part(B_N, IH + 5, nmp, True, False)
                wait(pe, convhi_ready, g + 1)
                wait(pe, convlo_ready, g + 1)
                part(B_R, IH, conv, False, True, gru_r_done)
                part(B_Z, IH + 2, conv, False, True, gru_z_done)
                part(B_N, IH + 4, conv, False, True, gru_n_done)

            def out_transposes(g):
                wait(pe, gru_ready, g + 1)
                for b in range(GB):
                    t = pe.transpose(bank[B_N][:, b * N:(b + 1) * N], gru[:, b * N:(b + 1) * N], ident[:, :])
                t.then_inc(outT_done, 1)

            c2_taps = c2_nat[:, :].rearrange("o (i k) -> o k i", k=TAPS)
            natural = [c1_nat[:, :]] + [c2_taps[:, k, :] for k in range(TAPS)] + [c2_sums[:, j, :] for j in range(HALF)]
            natural += [hh_nat[:, 0, :], hh_nat[:, 1, :], hhn_half[:, :]]
            natural += [ih_nat[:, gate, half * D:(half + 1) * D] for gate in range(3) for half in range(2)]

            def weight_transposes(c):
                earlier = [e for e in range(c) if chunk_bank[e] == chunk_bank[c]]
                if earlier:
                    pe.wait_ge(w_lo_ready, earlier[-1] + 1)
                for k, m in enumerate(chunks[c]):
                    t = pe.transpose(bank[chunk_bank[c]][:, k * D:(k + 1) * D], natural[m], ident[:, :])
                t.then_inc(wT_done, 1)

            pe.wait_ge(const_set, 4)
            pe.wait_ge(msgw_in, 16)
            pe.transpose(bank[B_F1][:, D:2 * D], msg_nat[:, :], ident[:, :]).then_inc(msgT_done, 1)
            pe.wait_ge(c1_in, 16)
            weight_transposes(0)
            pe.wait_ge(c2_in, 16)
            weight_transposes(1)
            h_transposes(0)
            pe.wait_ge(w_ms_ready, 1)
            pe.wait_ge(vecs_in, 16 * 11)
            pe.transpose(bank[B_F1][:, 0:NVEC], vecs[:, :], ident[0:NVEC, 0:NVEC]).then_inc(vecT_done, 1)
            weight_transposes(2)
            pe.wait_ge(w_ms_ready, 2)
            messages(0, 0)
            pe.wait_ge(w_hi_ready, 1)
            pe.wait_ge(w_lo_ready, 1)
            conv1(0, 0)
            weight_transposes(3)
            dist_transposes(0)
            weight_transposes(4)
            distances(0)
            pe.wait_ge(c2_sums_ready, 2)
            weight_transposes(5)
            weight_transposes(6)
            pe.wait_ge(hhn_ready, 1)
            pe.wait_ge(gruw_in, 32)
            for c in range(7, EARLY):
                weight_transposes(c)
            aggregate(0)
            pe.wait_ge(w_hi_ready, EARLY - 1)
            pe.wait_ge(w_lo_ready, EARLY - 1)

            def iteration(g, p, first, last):
                q = 1 - p
                if first:
                    conv2_taps(g, p, 0, 0, 4)
                    h_transposes(g + 1)
                else:
                    if not last:
                        h_transposes(g + 1)
                    conv2_taps(g, p, 0, 0, 4)
                if not last:
                    messages(g + 1, q)
                conv2_taps(g, p, 0, 4, 6)
                if not last:
                    conv1(g + 1, q)
                if first:
                    weight_transposes(EARLY)
                conv2_taps(g, p, 0, 6, 9)
                if first:
                    pe.wait_ge(w_hi_ready, EARLY)
                    pe.wait_ge(w_lo_ready, EARLY)
                conv2_taps(g, p, 1, 0, 4)
                if not last:
                    dist_transposes(g + 1)
                conv2_taps(g, p, 1, 4, 8)
                conv2_taps(g, p, 2, 0, 1)
                if not last:
                    distances(g + 1)
                if first:
                    weight_transposes(EARLY + 1)
                conv2_taps(g, p, 2, 1, 5)
                if not first:
                    out_transposes(g - 1)
                if not last:
                    aggregate(g + 1)
                conv2_taps(g, p, 2, 5, 9)
                if first:
                    pe.wait_ge(w_hi_ready, len(chunks))
                    pe.wait_ge(w_lo_ready, len(chunks))
                gru_products(g, p, first, last)

            groups(pe, iteration)
            out_transposes(NG - 1)


INPUTS = ["x", "adj"] + ["L0_gnn_" + n for n in (
    "w_se", "b_se", "conv1_w", "bn1_g", "bn1_b", "bn1_m", "bn1_v", "conv2_w", "bn2_g", "bn2_b", "bn2_m", "bn2_v",
    "w_msg", "b_msg", "w_ih", "b_ih", "w_hh", "b_hh")]


def kernel(**inputs):
    import numpy as np
    import concourse.bacc as bacc
    from concourse.bass_utils import run_bass_kernel_spmd

    nc = bacc.Bacc("TRN2", target_bir_lowering=False, num_devices=1)
    arrays, args = {}, []
    for name in INPUTS:
        a = np.ascontiguousarray(inputs[name])
        arrays[f"in_{name}"] = a
        args.append(nc.dram_tensor(f"in_{name}", a.shape, mybir.dt.from_np(a.dtype), kind="ExternalInput").ap())
    out = nc.dram_tensor("out", inputs["x"].shape, F32, kind="ExternalOutput").ap()
    gnn_block(nc, *args, out)
    return run_bass_kernel_spmd(nc, [arrays], core_ids=[0]).results[0]["out"]
```

```python
from contextlib import ExitStack

import concourse.bass as bass
from concourse import mybir

F32 = mybir.dt.float32
F32R = mybir.dt.float32r
BF16 = mybir.dt.bfloat16
ALU = mybir.AluOpType
ACT = mybir.ActivationFunctionType
AX = mybir.AxisListType

EPS = 1e-5
GB = 4
QUAD = 32


def gnn_block(nc, x, adj, w_se, b_se, conv1_w, bn1_g, bn1_b, bn1_m, bn1_v, conv2_w, bn2_g, bn2_b, bn2_m, bn2_v,
              w_msg, b_msg, w_ih, b_ih, w_hh, b_hh, out):
    NB, N, D = x.shape
    NSE = w_se.shape[0]
    TAPS = conv2_w.shape[2]
    HALF = TAPS // 2
    NG = NB // GB
    GC = GB * N
    MS = D + NSE + 1
    UN = N // 2 + 1
    NPAD = 2 * UN
    UOFF = 2
    UPAD = UN + 5

    def from_middle(j):
        return abs(j - HALF // 2)

    TAP_ORDER = [2 * j + e for e in range(2) for j in sorted(range(len(range(e, TAPS, 2))), key=from_middle)]

    ctx = ExitStack()
    with ctx:
        def sb(name, shape, dt=F32):
            return ctx.enter_context(nc.sbuf_tensor(name, shape, dt))

        def sem(name):
            return ctx.enter_context(nc.semaphore(name))

        NVEC = 14 + NSE
        vecs = sb("vecs", [NVEC, D])
        vcol = sb("vcol", [D, NVEC])
        bn_rstd = sb("bn_rstd", [D, 2])
        bn_scale = sb("bn_scale", [D, 2])
        bn_ms = sb("bn_ms", [D, 2])
        bn_shift = sb("bn_shift", [D, 2])
        gru_b = sb("gru_b", [D, 4])
        gru_s = sb("gru_s", [D, 2])
        bias_row = sb("bias_row", [N, MS])
        c1_nat = sb("c1_nat", [D, D])
        c2_nat = sb("c2_nat", [D, D * TAPS])
        c2_sums = sb("c2_sums", [D, HALF, D])
        msg_nat = sb("msg_nat", [D, D])
        ih_nat = sb("ih_nat", [D, 3, 2 * D])
        hh_nat = sb("hh_nat", [D, 3, D])
        CONV1, CONV2, SUMS, HH = 0, 1, 1 + TAPS, 1 + TAPS + HALF
        IH, NMAT = HH + 3, HH + 9
        w_hi = sb("w_hi", [D, NMAT, D], F32R)
        w_lo = sb("w_lo", [D, NMAT, D], F32R)
        w_ms = sb("w_ms", [D, MS])
        ident = sb("ident", [128, 128])
        ident_b = sb("ident_b", [128, 128], BF16)
        halves = sb("halves", [128, 8])
        quad_mask = sb("quad_mask", [128, GB, N], BF16)

        x_all = sb("x_all", [N, NB, D])
        adj_in = [sb(f"adj_in{p}", [N, GB, N]) for p in range(2)]
        adj_T = sb("adj_T", [N, GC])
        stats = sb("stats", [N, GB, 6])
        halves_sum = sb("halves_sum", [N, GB])
        halves_diff = sb("halves_diff", [N, GB])
        diff_sq = sb("diff_sq", [N, GB])
        sq_sum = sb("sq_sum", [N, GB])
        sq_mean = sb("sq_mean", [N, GB])
        mean = sb("mean", [N, GB])
        var_eps = sb("var_eps", [N, GB])
        rstd = sb("rstd", [N, GB])
        x_norm = sb("x_norm", [N, GB, D])
        h_f = [sb(f"h_f{p}", [D, GC]) for p in range(2)]
        h_hi = [sb(f"h_hi{p}", [D, GC], F32R) for p in range(2)]
        h_lo = [sb(f"h_lo{p}", [D, GC], F32R) for p in range(2)]
        h_s = sb("h_s", [D, GC])
        h_half = sb("h_half", [D, GC])
        a1_f = sb("a1_f", [D, GB, NPAD])
        a1_sum = sb("a1_sum", [D, GB, UN])
        a1_hi = [sb(f"a1_hi{p}", [D, 3, GB, UPAD], F32R) for p in range(2)]
        a1_lo = [sb(f"a1_lo{p}", [D, 3, GB, UPAD], F32R) for p in range(2)]
        ms_b = sb("ms_b", [N, GB, MS])
        msg = sb("msg", [N, GB, D])
        s_sq = sb("s_sq", [N, GB, NSE])
        emb = sb("emb", [N, GB, NSE + 1])
        emb_rest = sb("emb_rest", [N, GB, NSE + 1])
        emb_part = sb("emb_part", [N, GB, 3, NSE + 1], BF16)
        dist_l = sb("dist_l", [N, GB, QUAD], BF16)
        dist_r = sb("dist_r", [N, GB, QUAD], BF16)
        dist_lT = sb("dist_lT", [128, GB, N], BF16)
        dist_rT = sb("dist_rT", [128, N], BF16)
        edge = sb("edge", [N, GC])
        edge_m = sb("edge_m", [N, GC])
        nmp_hi = [sb(f"nmp_hi{p}", [D, GC], F32R) for p in range(2)]
        nmp_lo = [sb(f"nmp_lo{p}", [D, GC], F32R) for p in range(2)]
        q0 = sb("q0", [D, GB, UN])
        q1 = sb("q1", [D, GB, N // 2])
        h_q0 = sb("h_q0", [D, GB, N // 2])
        q01 = sb("q01", [D, GB, N // 2])
        h_q01 = sb("h_q01", [D, GB, N // 2])
        conv_f = sb("conv_f", [D, GC])
        conv_hi = sb("conv_hi", [D, GC], F32R)
        conv_lo = sb("conv_lo", [D, GC], F32R)
        t_r = sb("t_r", [D, GC])
        t_z = sb("t_z", [D, GC])
        hh_n = sb("hh_n", [D, GC])
        hn = sb("hn", [D, GC])
        n_pre = sb("n_pre", [D, GC])
        n_gate = sb("n_gate", [D, GC])
        z_h = sb("z_h", [D, GC])
        z_n = sb("z_n", [D, GC])
        gru = sb("gru", [D, GC])
        y = [sb(f"y{p}", [N, GB, D]) for p in range(2)]

        bank = [ctx.enter_context(nc.psum_tensor(f"bank{k}", [128, GC], F32)) for k in range(8)]
        B_CA, B_CB, B_R, B_Z, B_HN, B_N, B_F0, B_F1 = range(8)

        vecs_in, vecs_in_pool, msgw_in, c1_in, c2_in, gruw_in, bias_in = (sem(n) for n in (
            "vecs_in", "vecs_in_pool", "msgw_in", "c1_in", "c2_in", "gruw_in", "bias_in"))
        x_in = [sem(f"x_in{p}") for p in range(2)]
        adj_in_sem = [sem(f"adj_in_sem{p}") for p in range(2)]
        out_done = [sem(f"out_done{p}") for p in range(2)]
        const_set = sem("const_set")
        dve_const = sem("dve_const")
        vecT_done, vcol_ready, bn_rstd_ready, bn_chain = (sem(n) for n in (
            "vecT_done", "vcol_ready", "bn_rstd_ready", "bn_chain"))
        c2_sums_ready = sem("c2_sums_ready")
        msgT_done, w_ms_ready = sem("msgT_done"), sem("w_ms_ready")
        wT_done, w_hi_ready, w_lo_ready = sem("wT_done"), sem("w_hi_ready"), sem("w_lo_ready")
        stats_ready = sem("stats_ready")
        parts_ready = sem("parts_ready")
        parts2_ready = sem("parts2_ready")
        mean_ready = sem("mean_ready")
        vareps_ready = sem("vareps_ready")
        rstd_ready = sem("rstd_ready")
        xnorm_ready = sem("xnorm_ready")
        hT_done = sem("hT_done")
        hf_ready, hhi_ready, hlo_ready = sem("hf_ready"), sem("hhi_ready"), sem("hlo_ready")
        conv1_done = sem("conv1_done")
        hs_ready, hhalf_ready = sem("hs_ready"), sem("hhalf_ready")
        a1f_ready, a1hi_ready, a1lo_ready = sem("a1f_ready"), sem("a1hi_ready"), sem("a1lo_ready")
        a1sum_ready, a1shi_ready, a1slo_ready = sem("a1sum_ready"), sem("a1shi_ready"), sem("a1slo_ready")
        msg_done = sem("msg_done")
        msb_ready = sem("msb_ready")
        msg_ready = sem("msg_ready")
        ssq_ready, emb_ready = sem("ssq_ready"), sem("emb_ready")
        part_ready, rest_ready = sem("part_ready"), sem("rest_ready")
        dist_in_ready = sem("dist_in_ready")
        distT_done = sem("distT_done")
        dlT_ready, drT_ready = sem("dlT_ready"), sem("drT_ready")
        adjT_ready = sem("adjT_ready")
        dist_done = sem("dist_done")
        edge_ready, edgem_ready = sem("edge_ready"), sem("edgem_ready")
        nmp_done, nmphi_ready, nmplo_ready = sem("nmp_done"), sem("nmphi_ready"), sem("nmplo_ready")
        q0_done, q1_done, q2_done = sem("q0_done"), sem("q1_done"), sem("q2_done")
        q0_ready, q1_ready = sem("q0_ready"), sem("q1_ready")
        hq0_ready, q01_ready, hq01_ready = sem("hq0_ready"), sem("q01_ready"), sem("hq01_ready")
        convf_ready, convhi_ready, convlo_ready = sem("convf_ready"), sem("convhi_ready"), sem("convlo_ready")
        gru_hn_done, gru_r_done, gru_z_done, gru_n_done = (sem(n) for n in (
            "gru_hn_done", "gru_r_done", "gru_z_done", "gru_n_done"))
        tr_ready, tz_ready, hhn_ready, hn_ready, npre_ready = (sem(n) for n in (
            "tr_ready", "tz_ready", "hhn_ready", "hn_ready", "npre_ready"))
        zh_ready, ngate_ready, zn_ready, gru_ready = (sem(n) for n in (
            "zh_ready", "ngate_ready", "zn_ready", "gru_ready"))
        outT_done, y_ready = sem("outT_done"), sem("y_ready")

        def wait(eng, s, value):
            if not (isinstance(value, int) and value <= 0):
                eng.wait_ge(s, value)

        def moved(g, p):
            return 8 * g + 16 - 8 * p

        def groups(eng, iteration):
            iteration(1, 1, False)
            with eng.Fori(1, NG // 2 - 1) as pair:
                iteration(2 * pair, 0, False)
                iteration(2 * pair + 1, 1, False)
            iteration(NG - 2, 0, False)
            iteration(NG - 1, 1, True)

        def column_parts(last):
            if not last:
                return [(0, slice(0, GC))]
            return [(k, slice(k * GC // 2, (k + 1) * GC // 2)) for k in range(2)]

        def by_graph(ap):
            return ap.rearrange("p (b n) -> p b n", b=GB)

        def pairs_out(ap):
            return ap.rearrange("p (b u e) -> p b u e", b=GB, e=2)

        chunks = [[CONV1]] + [list(range(k, min(k + GB, NMAT))) for k in range(CONV2, NMAT, GB)]
        EVEN_CHUNKS = sum(c[0] < CONV2 + HALF for c in chunks)
        TAP_CHUNKS = sum(c[0] < SUMS for c in chunks)
        SUM_CHUNKS = sum(c[0] < HH for c in chunks)
        chunk_bank = [(B_R, B_CB, B_N)[c % 3] if c < TAP_CHUNKS else (B_R, B_N)[c % 2] for c in range(len(chunks))]

        PAIRS = [(a, b) for a in range(3) for b in range(3 - a)]
        EMB = NSE + 1
        ONE_SLOT = len(PAIRS) * EMB
        DIST_OPS = 3 + 3 + 1
        DVE_CONSTS = 2 * 4 + 1 + 2 + 1 + 2 + 3 + GB
        QCOLS = (UN + 1, N // 2, N // 2)

        R_BANKS, Z_BANKS, N_BANKS, LAST_OUT_BANKS = (B_R, B_F0), (B_Z, B_F1), (B_N, B_CA), (B_HN, B_CB)

        def conv_bank(p, k):
            return (B_CA, B_CB)[(p + k) % 2]

        block = ctx.enter_context(nc.Block())

        @block.sync
        def _(sp):
            def load_adj(g, p):
                for i in range(N // QUAD):
                    rows = slice(i * QUAD, (i + 1) * QUAD)
                    src = adj[bass.ds(g * GB, GB), :, rows].rearrange("b (j c) a -> c b j a", c=QUAD)
                    sp.dma_start(adj_in[p][rows, :, :].rearrange("c b (j a) -> c b j a", a=QUAD), src
                                 ).then_inc(adj_in_sem[p], 16)

            sp.dma_start(x_all[:, 0:GB, :], x[0:GB].rearrange("b n d -> n b d")).then_inc(x_in[0], 16)
            sp.dma_start(c1_nat[:, :], conv1_w.rearrange("o i k -> o (i k)")).then_inc(c1_in, 16)
            sp.dma_start(x_all[:, GB:2 * GB, :], x[GB:2 * GB].rearrange("b n d -> n b d")).then_inc(x_in[1], 16)
            for row, src in enumerate((bn1_g, bn1_b, bn1_m, bn1_v, bn2_g, bn2_b, bn2_m)):
                sp.dma_start(vecs[row:row + 1, :], src.rearrange("(a d) -> a d", a=1)).then_inc(vecs_in, 16)
            load_adj(0, 0)
            sp.dma_start(hh_nat[:, :, :], w_hh.rearrange("(a o) i -> o a i", a=3)).then_inc(gruw_in, 16)
            sp.dma_start(ih_nat[:, :, :], w_ih.rearrange("(a o) i -> o a i", a=3)).then_inc(gruw_in, 16)
            load_adj(1, 1)

            def load_ahead(g, p):
                wait(sp, x_in[p], moved(g, p))
                sp.dma_start(x_all[:, bass.ds((g + 2) * GB, GB), :],
                             x[bass.ds((g + 2) * GB, GB)].rearrange("b n d -> n b d")).then_inc(x_in[p], 16)
                wait(sp, adjT_ready, g + 1)
                load_adj(g + 2, p)

            def iteration(g, p, last):
                if not (isinstance(g, int) and g + 2 >= NG):
                    load_ahead(g, p)
                wait(sp, y_ready, g)
                sp.dma_start(out[bass.ds((g - 1) * GB, GB)].rearrange("b n d -> n b d"), y[1 - p][:, :, :]
                             ).then_inc(out_done[1 - p], 16)

            load_ahead(0, 0)
            groups(sp, iteration)
            for k, cols in column_parts(True):
                sp.wait_ge(y_ready, NG + k)
                graphs = slice(cols.start // N, cols.stop // N)
                sp.dma_start(out[(NG - 1) * GB + graphs.start:(NG - 1) * GB + graphs.stop].rearrange("b n d -> n b d"),
                             y[(NG - 1) % 2][:, graphs, :]).then_inc(out_done[(NG - 1) % 2], 16)
            for p in range(2):
                sp.wait_ge(out_done[p], 16 * (NG // 2 + p))

        @block.gpsimd
        def _(pool):
            pool.memset(ident[:, :], 0.0).then_inc(const_set, 1)
            pool.memset(halves[:, :], -0.5).then_inc(const_set, 1)
            pool.wait_ge(const_set, 2)
            pool.affine_select(out=ident[:, :], in_=ident[:, :], compare_op=ALU.not_equal, fill=1.0, base=0,
                               pattern=[[-1, 128]], channel_multiplier=1).then_inc(const_set, 1)

            pool.wait_ge(const_set, 3)
            pool.tensor_copy(ident_b[:, :], ident[:, :]).then_inc(const_set, 1)
            pool.dma_start(vecs[7:8, :], bn2_v.rearrange("(a d) -> a d", a=1)).then_inc(vecs_in_pool, 16)
            pool.dma_start(vecs[8:11, :], b_ih.rearrange("(a d) -> a d", a=3)).then_inc(vecs_in_pool, 16)
            pool.dma_start(vecs[11:14, :], b_hh.rearrange("(a d) -> a d", a=3)).then_inc(vecs_in_pool, 16)

            def norm_rstd(g):
                wait(pool, vareps_ready, g + 1)
                pool.tensor_tensor(rstd[:, :], var_eps[:, :], halves[:, 0:GB], ALU.pow).then_inc(rstd_ready, 1)

            def conv_parts(g):
                h_even, h_odd = (pairs_out(h_s[:, :])[:, :, :, e] for e in range(2))
                wait(pool, hs_ready, g + 1)
                wait(pool, convf_ready, 2 * g)
                wait(pool, q0_ready, g + 1)
                pool.tensor_tensor(h_q0[:, :, :], h_even, q0[:, :, 0:N // 2], ALU.add).then_inc(hq0_ready, 1)
                wait(pool, q1_ready, g + 1)
                pool.tensor_tensor(q01[:, :, :], q0[:, :, 1:UN], q1[:, :, :], ALU.add).then_inc(q01_ready, 1)
                wait(pool, q01_ready, g + 1)
                pool.tensor_tensor(h_q01[:, :, :], h_odd, q01[:, :, :], ALU.subtract).then_inc(hq01_ready, 1)

            taps_nat = c2_nat[:, :].rearrange("o (i k) -> o k i", k=TAPS)

            def tap_sums(half):
                js = slice(half * HALF // 2, (half + 1) * HALF // 2)
                pool.tensor_tensor(c2_sums[:, js, :], taps_nat[:, 0:TAPS - 1:2, :][:, js, :],
                                   taps_nat[:, 1:TAPS:2, :][:, js, :], ALU.add).then_inc(c2_sums_ready, 1)

            norm_rstd(0)
            pool.dma_start(bias_row[:, 0:D], b_msg.partition_broadcast(N)).then_inc(bias_in, 16)
            pool.dma_start(bias_row[:, D:D + NSE], b_se.partition_broadcast(N)).then_inc(bias_in, 16)
            pool.wait_ge(vcol_ready, 1)
            pool.tensor_scalar(bn_rstd[:, :], vcol[:, 3:8:4], EPS, None, ALU.add).then_inc(bn_rstd_ready, 1)
            pool.wait_ge(bn_rstd_ready, 1)
            pool.tensor_tensor(bn_rstd[:, :], bn_rstd[:, :], halves[:, 0:2], ALU.pow).then_inc(bn_rstd_ready, 1)
            pool.wait_ge(c2_in, 16)
            tap_sums(0)
            tap_sums(1)
            norm_rstd(1)
            conv_parts(0)
            norm_rstd(2)

            def iteration(g, p, last):
                conv_parts(g)
                if not (isinstance(g, int) and g + 2 >= NG):
                    norm_rstd(g + 2)

            groups(pool, iteration)

        @block.scalar
        def _(act):
            act.dma_start(msg_nat[:, :], w_msg).then_inc(msgw_in, 16)
            act.dma_start(c2_nat[:, :], conv2_w.rearrange("o i k -> o (i k)")).then_inc(c2_in, 16)
            act.dma_start(vecs[14:NVEC, :], w_se).then_inc(vecs_in, 16)

            def weights_high(c):
                mats = chunks[c]
                act.wait_ge(wT_done, c + 1)
                act.activation(w_hi[:, mats[0]:mats[-1] + 1, :], bank[chunk_bank[c]][:, 0:len(mats) * D],
                               ACT.Copy).then_inc(w_hi_ready, 1)

            def h_copies(g, p):
                wait(act, hT_done, g + 1)
                wait(act, msg_done, 2 * (g - 1))
                wait(act, hlo_ready, g - 1)
                act.activation(h_f[p][:, :], bank[B_F0][:, :], ACT.Relu).then_inc(hf_ready, 1)
                wait(act, hf_ready, g + 1)
                act.activation(h_hi[p][:, :], h_f[p][:, :], ACT.Copy).then_inc(hhi_ready, 1)

            def conv1_out(g):
                wait(act, conv1_done, g + 1)
                wait(act, a1lo_ready, g)
                wait(act, a1sum_ready, g)
                act.activation(a1_f[:, :, 1:N + 1], by_graph(bank[B_F1][:, :]), ACT.Relu, bias=bn_shift[:, 0:1],
                               scale=bn_scale[:, 0:1]).then_inc(a1f_ready, 1)

            def a1_high(g, p):
                wait(act, a1f_ready, g + 1)
                wait(act, q2_done, g - 1)
                act.activation(a1_hi[p][:, 0:2, :, UOFF:UOFF + UN],
                               a1_f[:, :, :].rearrange("p b (u e) -> p e b u", e=2), ACT.Copy).then_inc(a1hi_ready, 1)

            def a1_sum_high(g, p):
                wait(act, a1sum_ready, g + 1)
                act.activation(a1_hi[p][:, 2, :, UOFF:UOFF + UN], a1_sum[:, :, :], ACT.Copy).then_inc(a1shi_ready, 1)

            def message_relu(g):
                wait(act, msb_ready, 2 * (g + 1))
                wait(act, nmp_done, g)
                act.activation(msg[:, :, :], ms_b[:, :, 0:D], ACT.Relu).then_inc(msg_ready, 1)

            def dist_right(g):
                wait(act, distT_done, g + 1)
                wait(act, dist_done, g)
                act.activation(dist_rT[:, :], bank[B_F1][:, 0:N // 2].bitcast(BF16), ACT.Copy).then_inc(drT_ready, 1)

            def edges(g):
                wait(act, dist_done, g + 1)
                wait(act, edgem_ready, g)
                act.activation(edge[:, :], bank[B_Z][:, :], ACT.Exp).then_inc(edge_ready, 1)

            def nmp_high(g, p):
                wait(act, nmp_done, g + 1)
                wait(act, gru_n_done, g - 1)
                act.activation(nmp_hi[p][:, :], bank[B_F0][:, :], ACT.Copy).then_inc(nmphi_ready, 1)

            def h_shifted(g, p):
                wait(act, hq01_ready, g)
                act.activation(h_s[:, :], h_f[p][:, :], ACT.Identity, bias=bn_shift[:, 1:2]).then_inc(hs_ready, 1)
                wait(act, zh_ready, g)
                act.activation(h_half[:, :], h_f[p][:, :], ACT.Copy, scale=0.5).then_inc(hhalf_ready, 1)

            def q0_scaled(g, p):
                wait(act, q0_done, g + 1)
                wait(act, hq01_ready, g)
                src = bank[conv_bank(p, 0)][:, 0:GB * QCOLS[0]].rearrange("p (b u) -> p b u", b=GB)
                act.activation(q0[:, :, :], src[:, :, 0:UN], ACT.Copy, scale=bn_scale[:, 1:2]).then_inc(q0_ready, 1)

            def q1_scaled(g, p):
                wait(act, q1_done, g + 1)
                wait(act, convf_ready, 2 * g)
                src = bank[conv_bank(p, 1)][:, 0:GB * QCOLS[1]].rearrange("p (b u) -> p b u", b=GB)
                act.activation(q1[:, :, :], src, ACT.Copy, scale=bn_scale[:, 1:2]).then_inc(q1_ready, 1)

            def conv_high(g):
                wait(act, convf_ready, 2 * (g + 1))
                wait(act, gru_n_done, g)
                act.activation(conv_hi[:, :], conv_f[:, :], ACT.Relu).then_inc(convhi_ready, 1)

            def hh_n_half(g):
                wait(act, gru_hn_done, g + 1)
                wait(act, hn_ready, g)
                act.activation(hh_n[:, :], bank[B_HN][:, :], ACT.Identity, bias=gru_b[:, 2:3], scale=0.5
                               ).then_inc(hhn_ready, 1)

            def gate_r(g, k, cols):
                wait(act, gru_r_done, g + 1 + k)
                wait(act, hn_ready, g)
                act.activation(t_r[:, cols], bank[R_BANKS[k]][:, cols], ACT.Tanh, bias=gru_b[:, 0:1], scale=0.5
                               ).then_inc(tr_ready, 1)

            def gate_z(g, k, cols):
                wait(act, gru_z_done, g + 1 + k)
                wait(act, zn_ready, g)
                act.activation(t_z[:, cols], bank[Z_BANKS[k]][:, cols], ACT.Tanh, bias=gru_b[:, 1:2], scale=0.5
                               ).then_inc(tz_ready, 1)

            def gate_n(g, k, cols):
                wait(act, npre_ready, g + 1 + k)
                wait(act, gru_ready, g)
                act.activation(n_gate[:, cols], n_pre[:, cols], ACT.Tanh, bias=gru_b[:, 3:4]).then_inc(ngate_ready, 1)

            weights_high(0)
            h_copies(0, 0)
            weights_high(1)
            act.wait_ge(bn_chain, 7)
            act.wait_ge(dve_const, DVE_CONSTS)
            weights_high(2)
            conv1_out(0)
            a1_high(0, 0)
            weights_high(3)
            weights_high(4)
            message_relu(0)
            a1_sum_high(0, 0)
            weights_high(5)
            dist_right(0)
            edges(0)
            weights_high(6)
            q0_scaled(0, 0)
            nmp_high(0, 0)
            weights_high(7)
            h_copies(1, 1)
            weights_high(8)
            h_shifted(0, 0)
            q1_scaled(0, 0)
            conv1_out(1)
            a1_high(1, 1)
            dist_right(1)
            weights_high(9)
            message_relu(1)
            a1_sum_high(1, 1)
            edges(1)
            conv_high(0)
            nmp_high(1, 1)
            hh_n_half(0)

            def iteration(g, p, last):
                q = 1 - p
                gate_r(g - 1, 0, slice(0, GC))
                gate_z(g - 1, 0, slice(0, GC))
                if not last:
                    h_copies(g + 1, q)
                gate_n(g - 1, 0, slice(0, GC))
                if not last:
                    conv1_out(g + 1)
                    a1_high(g + 1, q)
                    message_relu(g + 1)
                    dist_right(g + 1)
                q0_scaled(g, p)
                if not last:
                    edges(g + 1)
                h_shifted(g, p)
                q1_scaled(g, p)
                if not last:
                    a1_sum_high(g + 1, q)
                    nmp_high(g + 1, q)
                conv_high(g)
                hh_n_half(g)

            groups(act, iteration)
            first_half, second_half = column_parts(True)
            gate_r(NG - 1, *first_half)
            gate_z(NG - 1, *first_half)
            gate_r(NG - 1, *second_half)
            gate_n(NG - 1, *first_half)
            gate_z(NG - 1, *second_half)
            gate_n(NG - 1, *second_half)

        @block.vector
        def _(dve):
            for t in a1_hi + a1_lo:
                dve.memset(t[:, :, :, 0:UOFF].bitcast(F32), 0.0).then_inc(dve_const, 1)
                dve.memset(t[:, :, :, UOFF + UN:UPAD].bitcast(F32), 0.0).then_inc(dve_const, 1)
            dve.memset(a1_f[:, :, 0:NPAD:NPAD - 1], 0.0).then_inc(dve_const, 1)
            for t in (dist_l, dist_r):
                dve.memset(t[:, :, :], 0.0).then_inc(dve_const, 1)
            dve.memset(quad_mask[:, :, :], 0.0).then_inc(dve_const, 1)
            dve.memset(w_ms[:, D + NSE:MS], 0.0).then_inc(dve_const, 1)
            dve.memset(bias_row[:, D + NSE:MS], 0.0).then_inc(dve_const, 1)
            dve.wait_ge(dve_const, DVE_CONSTS - 4 - GB)
            dve.memset(dist_l[:, :, ONE_SLOT:ONE_SLOT + 3], 1.0).then_inc(dve_const, 1)
            for k, (a, b) in enumerate(PAIRS):
                if b == 0:
                    dve.memset(dist_r[:, :, k * EMB + NSE], -1.0).then_inc(dve_const, 1)
            for b in range(GB):
                dve.memset(quad_mask[b * QUAD:(b + 1) * QUAD, b, :], 1.0).then_inc(dve_const, 1)

            def half_stats(g, p):
                wait(dve, x_in[p], moved(g, p))
                for b in range(GB):
                    dve.bn_stats(stats[:, b, :], x_all[:, bass.ds(g * GB + b, 1), :]).then_inc(stats_ready, 1)

            def x_moments(g):
                wait(dve, stats_ready, GB * (g + 1))
                even, odd = stats[:, :, 1], stats[:, :, 4]
                dve.tensor_tensor(halves_sum[:, :], even, odd, ALU.add).then_inc(parts_ready, 1)
                dve.tensor_tensor(halves_diff[:, :], even, odd, ALU.subtract).then_inc(parts_ready, 1)
                dve.tensor_tensor(sq_sum[:, :], stats[:, :, 2], stats[:, :, 5], ALU.add).then_inc(parts_ready, 1)
                wait(dve, parts_ready, 3 * (g + 1))
                dve.tensor_tensor(diff_sq[:, :], halves_diff[:, :], halves_diff[:, :], ALU.mult
                                  ).then_inc(parts2_ready, 1)
                dve.tensor_scalar(sq_mean[:, :], sq_sum[:, :], 1.0 / D, EPS, ALU.mult, ALU.add
                                  ).then_inc(parts2_ready, 1)
                dve.tensor_scalar(mean[:, :], halves_sum[:, :], 0.5, None, ALU.mult).then_inc(mean_ready, 1)
                wait(dve, parts2_ready, 2 * (g + 1))
                dve.scalar_tensor_tensor(var_eps[:, :], diff_sq[:, :], 0.25, sq_mean[:, :], ALU.mult, ALU.add
                                         ).then_inc(vareps_ready, 1)

            def x_stats(g, p):
                half_stats(g, p)
                x_moments(g)

            def x_normed(g):
                wait(dve, mean_ready, g + 1)
                wait(dve, rstd_ready, g + 1)
                for b in range(GB):
                    dve.tensor_scalar(x_norm[:, b:b + 1, :], x_all[:, bass.ds(g * GB + b, 1), :],
                                      mean[:, b:b + 1], rstd[:, b:b + 1], ALU.subtract, ALU.mult
                                      ).then_inc(xnorm_ready, 1)

            def h_low(g, p):
                wait(dve, hhi_ready, g + 1)
                dve.tensor_tensor(h_lo[p][:, :], h_f[p][:, :], h_hi[p][:, :].bitcast(F32), ALU.subtract
                                  ).then_inc(hlo_ready, 1)

            def a1_low(g, p):
                wait(dve, a1hi_ready, g + 1)
                for e in range(2):
                    low = dve.tensor_tensor(a1_lo[p][:, e, :, UOFF:UOFF + UN], a1_f[:, :, e:NPAD:2],
                                            a1_hi[p][:, e, :, UOFF:UOFF + UN].bitcast(F32), ALU.subtract)
                low.then_inc(a1lo_ready, 1)
                wait(dve, a1slo_ready, g)
                dve.tensor_tensor(a1_sum[:, :, :], a1_f[:, :, 0:NPAD:2], a1_f[:, :, 1:NPAD:2], ALU.add
                                  ).then_inc(a1sum_ready, 1)

            def a1_sum_low(g, p):
                wait(dve, a1shi_ready, g + 1)
                dve.tensor_tensor(a1_lo[p][:, 2, :, UOFF:UOFF + UN], a1_sum[:, :, :],
                                  a1_hi[p][:, 2, :, UOFF:UOFF + UN].bitcast(F32), ALU.subtract
                                  ).then_inc(a1slo_ready, 1)

            def messages(g):
                half = GB // 2
                wait(dve, msg_ready, g)
                for k, src in enumerate((B_HN, B_F0)):
                    wait(dve, msg_done, 2 * g + k + 1)
                    dve.tensor_tensor(ms_b[:, k * half:(k + 1) * half, :],
                                      bank[src][:, 0:half * MS].rearrange("p (b m) -> p b m", b=half),
                                      bias_row[:, :].unsqueeze(1).broadcast_to([N, half, MS]), ALU.add
                                      ).then_inc(msb_ready, 1)

            def dist_sides(g):
                e = ms_b[:, :, D:D + NSE]
                wait(dve, msb_ready, 2 * (g + 1))
                dve.tensor_tensor(s_sq[:, :, :], e, e, ALU.mult).then_inc(ssq_ready, 1)
                dve.tensor_copy(emb[:, :, 0:NSE], e).then_inc(emb_ready, 1)
                wait(dve, ssq_ready, g + 1)
                dve.tensor_reduce(emb[:, :, NSE:EMB], s_sq[:, :, :], AX.X, ALU.add).then_inc(emb_ready, 1)
                wait(dve, emb_ready, 2 * (g + 1))
                dve.tensor_copy(emb_part[:, :, 0, :], emb[:, :, :]).then_inc(part_ready, 1)
                wait(dve, part_ready, 3 * g + 1)
                dve.tensor_tensor(emb_rest[:, :, :], emb[:, :, :], emb_part[:, :, 0, :], ALU.subtract
                                  ).then_inc(rest_ready, 1)
                dve.tensor_copy(dist_l[:, :, 0:3 * EMB].rearrange("n b (k e) -> n b k e", k=3),
                                emb_part[:, :, 0:1, :].broadcast_to([N, GB, 3, EMB])).then_inc(dist_in_ready, 1)
                wait(dve, rest_ready, g + 1)
                dve.tensor_copy(emb_part[:, :, 1, :], emb_rest[:, :, :]).then_inc(part_ready, 1)
                wait(dve, part_ready, 3 * g + 2)
                dve.tensor_tensor(emb_part[:, :, 2, :], emb_rest[:, :, :], emb_part[:, :, 1, :], ALU.subtract
                                  ).then_inc(part_ready, 1)
                dve.tensor_copy(dist_l[:, :, 3 * EMB:5 * EMB].rearrange("n b (k e) -> n b k e", k=2),
                                emb_part[:, :, 1:2, :].broadcast_to([N, GB, 2, EMB])).then_inc(dist_in_ready, 1)
                right = dist_r[:, :, 0:6 * EMB].rearrange("n b (k e) -> n b k e", k=6)
                dve.tensor_scalar(right[:, :, 3:5, 0:NSE], emb_part[:, :, 0:2, 0:NSE], 2.0, None, ALU.mult
                                  ).then_inc(dist_in_ready, 1)
                dve.tensor_scalar(right[:, :, 5, 0:NSE], emb_part[:, :, 0, 0:NSE], 2.0, None, ALU.mult
                                  ).then_inc(dist_in_ready, 1)
                wait(dve, part_ready, 3 * (g + 1))
                dve.tensor_copy(dist_l[:, :, 5 * EMB:6 * EMB], emb_part[:, :, 2, :]).then_inc(dist_in_ready, 1)
                dve.tensor_scalar(right[:, :, 0:3, 0:NSE], emb_part[:, :, :, 0:NSE], 2.0, None, ALU.mult
                                  ).then_inc(dist_in_ready, 1)
                dve.tensor_scalar(dist_r[:, :, ONE_SLOT:ONE_SLOT + 3], emb_part[:, :, :, NSE], -1.0, None, ALU.mult
                                  ).then_inc(dist_in_ready, 1)

            def dist_left(g):
                wait(dve, distT_done, g + 1)
                dve.tensor_tensor(dist_lT[:, :, :], bank[B_F0][:, 0:N // 2].bitcast(BF16).unsqueeze(1).broadcast_to([128, GB, N]),
                                  quad_mask[:, :, :], ALU.mult).then_inc(dlT_ready, 1)

            def adj_transposed(g, p):
                wait(dve, adj_in_sem[p], N // QUAD * moved(g, p))
                dve.transpose(adj_T[:, :], adj_in[p][:, :, :].rearrange("n b m -> n (b m)")).then_inc(adjT_ready, 1)

            def masked_edges(g):
                wait(dve, adjT_ready, g + 1)
                wait(dve, edge_ready, g + 1)
                dve.tensor_tensor(edge_m[:, :], adj_T[:, :], edge[:, :], ALU.mult).then_inc(edgem_ready, 1)

            def nmp_low(g, p):
                wait(dve, nmphi_ready, g + 1)
                dve.tensor_tensor(nmp_lo[p][:, :], bank[B_F0][:, :], nmp_hi[p][:, :].bitcast(F32), ALU.subtract
                                  ).then_inc(nmplo_ready, 1)

            def conv_even(g):
                wait(dve, hq0_ready, g + 1)
                wait(dve, q1_ready, g + 1)
                dve.tensor_tensor(pairs_out(conv_f[:, :])[:, :, :, 0], h_q0[:, :, :], q1[:, :, :], ALU.add
                                  ).then_inc(convf_ready, 1)

            def conv_odd(g, p):
                wait(dve, hq01_ready, g + 1)
                wait(dve, q2_done, g + 1)
                src = bank[conv_bank(p, 2)][:, 0:GB * QCOLS[2]].rearrange("p (b u) -> p b u", b=GB)
                dve.scalar_tensor_tensor(pairs_out(conv_f[:, :])[:, :, :, 1], src, bn_scale[:, 1:2], h_q01[:, :, :],
                                         ALU.mult, ALU.add).then_inc(convf_ready, 1)

            def conv_low(g):
                wait(dve, convhi_ready, g + 1)
                dve.scalar_tensor_tensor(conv_lo[:, :], conv_f[:, :], 0.0, conv_hi[:, :].bitcast(F32),
                                         ALU.max, ALU.subtract).then_inc(convlo_ready, 1)

            def n_hidden(g, k, cols):
                wait(dve, tr_ready, g + 1 + k)
                wait(dve, hhn_ready, g + 1)
                dve.scalar_tensor_tensor(hn[:, cols], t_r[:, cols], 1.0, hh_n[:, cols], ALU.add, ALU.mult
                                         ).then_inc(hn_ready, 1)

            def n_argument(g, k, cols):
                wait(dve, gru_n_done, g + 1 + k)
                wait(dve, hn_ready, g + 1 + k)
                dve.tensor_tensor(n_pre[:, cols], bank[N_BANKS[k]][:, cols], hn[:, cols], ALU.add).then_inc(npre_ready, 1)

            def z_times_h(g, k, cols):
                wait(dve, tz_ready, g + 1 + k)
                wait(dve, hhalf_ready, g + 1)
                dve.scalar_tensor_tensor(z_h[:, cols], t_z[:, cols], 1.0, h_half[:, cols], ALU.add, ALU.mult
                                         ).then_inc(zh_ready, 1)

            def z_times_n(g, k, cols):
                wait(dve, ngate_ready, g + 1 + k)
                dve.scalar_tensor_tensor(z_n[:, cols], t_z[:, cols], 1.0, n_gate[:, cols], ALU.subtract, ALU.mult
                                         ).then_inc(zn_ready, 1)

            def gates_out(g, k, cols):
                wait(dve, zh_ready, g + 1 + k)
                wait(dve, zn_ready, g + 1 + k)
                dve.scalar_tensor_tensor(gru[:, cols], z_n[:, cols], -0.5, z_h[:, cols], ALU.mult, ALU.add
                                         ).then_inc(gru_ready, 1)

            def result(g, p, k, cols, src):
                graphs = slice(cols.start // N, cols.stop // N)
                wait(dve, outT_done, g + 1 + k)
                wait(dve, out_done[p], moved(g, p) - 16)
                dve.tensor_tensor(y[p][:, graphs, :], bank[src][:, cols].rearrange("p (b d) -> p b d", d=D),
                                  x_all[:, bass.ds(g * GB + graphs.start, graphs.stop - graphs.start), :], ALU.add
                                  ).then_inc(y_ready, 1)

            def weights_low(c):
                part = slice(chunks[c][0], chunks[c][-1] + 1)
                dve.wait_ge(w_hi_ready, c + 1)
                dve.tensor_tensor(w_lo[:, part, :],
                                  bank[chunk_bank[c]][:, 0:len(chunks[c]) * D].rearrange("p (m d) -> p m d", d=D),
                                  w_hi[:, part, :].bitcast(F32), ALU.subtract).then_inc(w_lo_ready, 1)

            x_stats(0, 0)
            dve.wait_ge(msgT_done, 1)
            dve.tensor_copy(w_ms[:, 0:D], bank[B_F1][:, D:2 * D]).then_inc(w_ms_ready, 1)
            weights_low(0)
            x_normed(0)
            half_stats(1, 1)
            dve.wait_ge(vecT_done, 1)
            dve.tensor_copy(vcol[:, :], bank[B_F1][:, 0:NVEC]).then_inc(vcol_ready, 1)
            dve.wait_ge(vcol_ready, 1)
            dve.tensor_copy(w_ms[:, D:D + NSE], vcol[:, 14:NVEC]).then_inc(w_ms_ready, 1)
            dve.tensor_tensor(gru_s[:, :], vcol[:, 8:10], vcol[:, 11:13], ALU.add).then_inc(bn_chain, 1)
            dve.tensor_scalar(gru_b[:, 2:3], vcol[:, 13:14], 0.5, None, ALU.mult).then_inc(bn_chain, 1)
            dve.tensor_copy(gru_b[:, 3:4], vcol[:, 10:11]).then_inc(bn_chain, 1)
            dve.wait_ge(bn_chain, 3)
            dve.tensor_scalar(gru_b[:, 0:2], gru_s[:, :], 0.5, None, ALU.mult).then_inc(bn_chain, 1)
            h_low(0, 0)
            dve.wait_ge(bn_rstd_ready, 2)
            dve.tensor_tensor(bn_scale[:, :], vcol[:, 0:8:4], bn_rstd[:, :], ALU.mult).then_inc(bn_chain, 1)
            dve.wait_ge(bn_chain, 5)
            dve.tensor_tensor(bn_ms[:, :], vcol[:, 2:8:4], bn_scale[:, :], ALU.mult).then_inc(bn_chain, 1)
            dve.wait_ge(bn_chain, 6)
            dve.tensor_tensor(bn_shift[:, :], vcol[:, 1:8:4], bn_ms[:, :], ALU.subtract).then_inc(bn_chain, 1)
            weights_low(1)
            dve.wait_ge(bias_in, 32)
            dve.wait_ge(dve_const, DVE_CONSTS)
            messages(0)
            weights_low(2)
            a1_low(0, 0)
            dist_sides(0)
            weights_low(3)
            weights_low(4)
            dist_left(0)
            adj_transposed(0, 0)
            x_moments(1)
            masked_edges(0)
            weights_low(5)
            a1_sum_low(0, 0)
            x_normed(1)
            nmp_low(0, 0)
            weights_low(6)
            weights_low(7)
            h_low(1, 1)
            messages(1)
            dist_sides(1)
            weights_low(8)
            dist_left(1)
            a1_low(1, 1)
            weights_low(9)
            conv_even(0)
            adj_transposed(1, 1)
            masked_edges(1)
            conv_odd(0, 0)
            half_stats(2, 0)
            conv_low(0)
            x_moments(2)
            a1_sum_low(1, 1)
            nmp_low(1, 1)
            x_normed(2)

            def iteration(g, p, last):
                q = 1 - p
                before_last_two = not (isinstance(g, int) and g + 2 >= NG)
                n_hidden(g - 1, 0, slice(0, GC))
                n_argument(g - 1, 0, slice(0, GC))
                z_times_h(g - 1, 0, slice(0, GC))
                if not last:
                    h_low(g + 1, q)
                    messages(g + 1)
                    dist_sides(g + 1)
                z_times_n(g - 1, 0, slice(0, GC))
                gates_out(g - 1, 0, slice(0, GC))
                if not last:
                    dist_left(g + 1)
                    a1_low(g + 1, q)
                    adj_transposed(g + 1, q)
                    masked_edges(g + 1)
                if before_last_two:
                    x_stats(g + 2, p)
                conv_even(g)
                if not last:
                    a1_sum_low(g + 1, q)
                conv_odd(g, p)
                result(g - 1, q, 0, slice(0, GC), B_N)
                conv_low(g)
                if not last:
                    nmp_low(g + 1, q)
                if before_last_two:
                    x_normed(g + 2)

            groups(dve, iteration)
            first_half, second_half = column_parts(True)
            last = (NG - 1, (NG - 1) % 2)
            n_hidden(NG - 1, *first_half)
            n_argument(NG - 1, *first_half)
            z_times_h(NG - 1, *first_half)
            n_hidden(NG - 1, *second_half)
            z_times_n(NG - 1, *first_half)
            n_argument(NG - 1, *second_half)
            z_times_h(NG - 1, *second_half)
            gates_out(NG - 1, *first_half)
            z_times_n(NG - 1, *second_half)
            gates_out(NG - 1, *second_half)
            result(*last, *first_half, LAST_OUT_BANKS[0])
            result(*last, *second_half, LAST_OUT_BANKS[1])

        @block.tensor
        def _(pe):
            def split_product(out, mat, hi, lo, start, stop, done=None):
                pe.matmul(out, w_hi[:, mat, :], hi, start=start, stop=False)
                pe.matmul(out, w_hi[:, mat, :], lo, start=False, stop=False)
                last = pe.matmul(out, w_lo[:, mat, :], hi, start=False, stop=stop)
                if done is not None:
                    last.then_inc(done, 1)

            def conv2_taps(g, p, k, first, last):
                parity = (0, 1, 0)[k]
                kind = (1, 0, 2)[k]
                have = ((0, UN - 1), (1, UN), (0, UN))[k]
                start = (0, 1, 1)[k]
                steps = len(range(parity, TAPS, 2))
                order = sorted(range(steps), key=from_middle)
                dst = bank[conv_bank(p, k)][:, 0:GB * QCOLS[k]].rearrange("p (b u) -> p b u", b=GB)
                if first == 0:
                    if k == 0:
                        wait(pe, a1hi_ready, g + 1)
                        wait(pe, a1lo_ready, g + 1)
                        wait(pe, q1_ready, g)
                    elif k == 1:
                        wait(pe, convf_ready, 2 * g)
                    else:
                        wait(pe, a1shi_ready, g + 1)
                        wait(pe, a1slo_ready, g + 1)
                        wait(pe, q0_ready, g + 1)
                for j in order[first:last]:
                    shift = j - HALF // 2
                    lo = max(0, have[0] - shift - start) // 2 * 2
                    hi = min(QCOLS[k], (have[1] - shift - start + 1) // 2 * 2)
                    if shift == 0:
                        lo, hi = 0, QCOLS[k]
                    cols = slice(lo + start + shift + UOFF, hi + start + shift + UOFF)
                    mat = SUMS + j if k == 2 and j < HALF else CONV2 + TAP_ORDER.index(2 * j + parity)
                    split_product(dst[:, :, lo:hi], mat, a1_hi[p][:, kind, :, cols], a1_lo[p][:, kind, :, cols],
                                  j == order[0], j == order[-1], (q0_done, q1_done, q2_done)[k]
                                  if j == order[-1] else None)

            def h_transposes(g):
                wait(pe, xnorm_ready, GB * (g + 1))
                wait(pe, nmplo_ready, g)
                for b in range(GB):
                    t = pe.transpose(bank[B_F0][:, b * N:(b + 1) * N], x_norm[:, b, :], ident[:, :])
                t.then_inc(hT_done, 1)

            def conv1(g, p):
                wait(pe, hhi_ready, g + 1)
                wait(pe, hlo_ready, g + 1)
                wait(pe, drT_ready, g)
                split_product(bank[B_F1][:, :], CONV1, h_hi[p][:, :], h_lo[p][:, :], True, True, conv1_done)

            def messages(g, p):
                half = GB // 2
                wait(pe, hf_ready, g + 1)
                wait(pe, hhn_ready, g - 1)
                for k, dst in enumerate((B_HN, B_F0)):
                    for b in range(half):
                        m = pe.matmul(bank[dst][:, b * MS:(b + 1) * MS],
                                      h_f[p][:, (k * half + b) * N:(k * half + b + 1) * N], w_ms[:, :],
                                      start=True, stop=True)
                    m.then_inc(msg_done, 1)

            def dist_transposes(g):
                wait(pe, dist_in_ready, DIST_OPS * (g + 1))
                wait(pe, a1f_ready, g + 1)
                pe.transpose(bank[B_F0][:, 0:N // 2].bitcast(BF16), dist_l[:, :, :].rearrange("n b k -> n (b k)"),
                             ident_b[:, :])
                pe.transpose(bank[B_F1][:, 0:N // 2].bitcast(BF16), dist_r[:, :, :].rearrange("n b k -> n (b k)"),
                             ident_b[:, :]
                             ).then_inc(distT_done, 1)

            def distances(g):
                wait(pe, dlT_ready, g + 1)
                wait(pe, drT_ready, g + 1)
                wait(pe, tz_ready, g - 1)
                for b in range(GB):
                    m = pe.matmul(bank[B_Z][:, b * N:(b + 1) * N], dist_lT[:, b, :], dist_rT[:, :],
                                  start=True, stop=True)
                m.then_inc(dist_done, 1)

            def aggregate(g):
                wait(pe, msg_ready, g + 1)
                wait(pe, edgem_ready, g + 1)
                wait(pe, dlT_ready, g + 1)
                for b in range(GB):
                    m = pe.matmul(bank[B_F0][:, b * N:(b + 1) * N], msg[:, b, :], edge_m[:, b * N:(b + 1) * N],
                                  start=True, stop=True)
                m.then_inc(nmp_done, 1)

            def gru_part(banks, mat, act, start, stop, parts, done=None):
                for k, cols in parts:
                    split_product(bank[banks[k]][:, cols], mat, act[0][:, cols], act[1][:, cols], start, stop, done)

            def gru_products(g, p, last, between=None):
                h, nmp, conv = (h_hi[p], h_lo[p]), (nmp_hi[p], nmp_lo[p]), (conv_hi, conv_lo)
                parts = column_parts(last)
                if not last:
                    wait(pe, msb_ready, 2 * (g + 2))
                else:
                    wait(pe, hhn_ready, g)
                gru_part((B_HN,), HH + 2, h, True, True, column_parts(False), gru_hn_done)
                wait(pe, tr_ready, g)
                wait(pe, nmplo_ready, g + 1)
                gru_part(R_BANKS, HH, h, True, False, parts)
                gru_part(R_BANKS, IH + 1, nmp, False, False, parts)
                if between is not None:
                    between()
                if not last:
                    wait(pe, edge_ready, g + 2)
                else:
                    wait(pe, tz_ready, g)
                    wait(pe, drT_ready, g + 1)
                gru_part(Z_BANKS, HH + 1, h, True, False, parts)
                gru_part(Z_BANKS, IH + 3, nmp, False, False, parts)
                wait(pe, y_ready, g)
                if last:
                    wait(pe, q1_ready, g + 1)
                gru_part(N_BANKS, IH + 5, nmp, True, False, parts)
                wait(pe, convhi_ready, g + 1)
                wait(pe, convlo_ready, g + 1)
                for part in parts:
                    gru_part(R_BANKS, IH, conv, False, True, [part], gru_r_done)
                    gru_part(Z_BANKS, IH + 2, conv, False, True, [part], gru_z_done)
                    gru_part(N_BANKS, IH + 4, conv, False, True, [part], gru_n_done)

            def out_transposes(g, k, cols, dst):
                wait(pe, gru_ready, g + 1 + k)
                for b in range(cols.start // N, cols.stop // N):
                    t = pe.transpose(bank[dst][:, b * N:(b + 1) * N], gru[:, b * N:(b + 1) * N], ident[:, :])
                t.then_inc(outT_done, 1)

            c2_taps = c2_nat[:, :].rearrange("o (i k) -> o k i", k=TAPS)
            natural = [c1_nat[:, :]] + [c2_taps[:, k, :] for k in TAP_ORDER] + [c2_sums[:, j, :] for j in range(HALF)]
            natural += [hh_nat[:, gate, :] for gate in range(3)]
            natural += [ih_nat[:, gate, half * D:(half + 1) * D] for gate in range(3) for half in range(2)]

            def weight_transposes(c):
                earlier = [e for e in range(c) if chunk_bank[e] == chunk_bank[c]]
                if earlier:
                    pe.wait_ge(w_lo_ready, earlier[-1] + 1)
                for k, m in enumerate(chunks[c]):
                    t = pe.transpose(bank[chunk_bank[c]][:, k * D:(k + 1) * D], natural[m], ident[:, :])
                t.then_inc(wT_done, 1)

            def split_done(count):
                pe.wait_ge(w_hi_ready, count)
                pe.wait_ge(w_lo_ready, count)

            def keep_warm(count):
                for _ in range(count):
                    pe.matmul(bank[B_CA][:, 0:128], ident[:, :], ident[:, :], start=True, stop=True)

            pe.wait_ge(const_set, 4)
            keep_warm(4)
            pe.wait_ge(msgw_in, 16)
            pe.transpose(bank[B_F1][:, D:2 * D], msg_nat[:, :], ident[:, :]).then_inc(msgT_done, 1)
            pe.wait_ge(c1_in, 16)
            weight_transposes(0)
            keep_warm(8)
            h_transposes(0)
            pe.wait_ge(w_ms_ready, 1)
            pe.wait_ge(vecs_in, 16 * 8)
            pe.wait_ge(vecs_in_pool, 16 * 3)
            pe.transpose(bank[B_F1][:, 0:NVEC], vecs[:, :], ident[0:NVEC, 0:NVEC]).then_inc(vecT_done, 1)
            pe.wait_ge(c2_in, 16)
            weight_transposes(1)
            pe.wait_ge(w_ms_ready, 2)
            messages(0, 0)
            weight_transposes(2)
            split_done(1)
            conv1(0, 0)
            weight_transposes(3)
            weight_transposes(4)
            pe.wait_ge(c2_sums_ready, 1)
            weight_transposes(5)
            split_done(EVEN_CHUNKS)
            conv2_taps(0, 0, 0, 0, 6)
            dist_transposes(0)
            conv2_taps(0, 0, 0, 6, 8)
            distances(0)
            split_done(EVEN_CHUNKS + 1)
            conv2_taps(0, 0, 0, 8, 9)
            pe.wait_ge(c2_sums_ready, 2)
            weight_transposes(6)
            split_done(TAP_CHUNKS - 1)
            conv2_taps(0, 0, 1, 0, 2)
            aggregate(0)
            split_done(TAP_CHUNKS)
            pe.wait_ge(gruw_in, 32)
            weight_transposes(7)
            conv2_taps(0, 0, 1, 2, 5)
            h_transposes(1)
            weight_transposes(8)
            conv2_taps(0, 0, 1, 5, 6)
            messages(1, 1)
            conv2_taps(0, 0, 1, 6, 8)
            split_done(SUM_CHUNKS)
            conv2_taps(0, 0, 2, 0, 2)
            conv1(1, 1)
            weight_transposes(9)
            conv2_taps(0, 0, 2, 2, 4)
            dist_transposes(1)
            conv2_taps(0, 0, 2, 4, 7)
            distances(1)
            conv2_taps(0, 0, 2, 7, 9)
            split_done(len(chunks))
            gru_products(0, 0, False, between=lambda: aggregate(1))

            def iteration(g, p, last):
                q = 1 - p
                if not last:
                    h_transposes(g + 1)
                conv2_taps(g, p, 0, 0, 4)
                if not last:
                    messages(g + 1, q)
                conv2_taps(g, p, 0, 4, 6)
                if not last:
                    conv1(g + 1, q)
                conv2_taps(g, p, 0, 6, 9)
                conv2_taps(g, p, 1, 0, 4)
                if not last:
                    dist_transposes(g + 1)
                conv2_taps(g, p, 1, 4, 8)
                conv2_taps(g, p, 2, 0, 1)
                if not last:
                    distances(g + 1)
                conv2_taps(g, p, 2, 1, 5)
                out_transposes(g - 1, 0, slice(0, GC), B_N)
                if not last:
                    aggregate(g + 1)
                conv2_taps(g, p, 2, 5, 9)
                gru_products(g, p, last)

            groups(pe, iteration)
            pe.wait_ge(hhn_ready, NG)
            pe.wait_ge(convf_ready, 2 * NG)
            for (k, cols), dst in zip(column_parts(True), LAST_OUT_BANKS):
                out_transposes(NG - 1, k, cols, dst)


INPUTS = ["x", "adj"] + ["L0_gnn_" + n for n in (
    "w_se", "b_se", "conv1_w", "bn1_g", "bn1_b", "bn1_m", "bn1_v", "conv2_w", "bn2_g", "bn2_b", "bn2_m", "bn2_v",
    "w_msg", "b_msg", "w_ih", "b_ih", "w_hh", "b_hh")]


def kernel(**inputs):
    import numpy as np
    import concourse.bacc as bacc
    from concourse.bass_utils import run_bass_kernel_spmd

    nc = bacc.Bacc("TRN2", target_bir_lowering=False, num_devices=1)
    arrays, args = {}, []
    for name in INPUTS:
        a = np.ascontiguousarray(inputs[name])
        arrays[f"in_{name}"] = a
        args.append(nc.dram_tensor(f"in_{name}", a.shape, mybir.dt.from_np(a.dtype), kind="ExternalInput").ap())
    out = nc.dram_tensor("out", inputs["x"].shape, F32, kind="ExternalOutput").ap()
    gnn_block(nc, *args, out)
    return run_bass_kernel_spmd(nc, [arrays], core_ids=[0]).results[0]["out"]
```
